# Optimizing a Trainium2 kernel written in Bass

```python
import numpy as np
import jax
import jax.numpy as jnp

def _softmax(x, axis=-1):
    return jax.nn.softmax(x, axis=axis)

def _gelu(x):
    return jax.nn.gelu(x, approximate=True)

def _silu(x):
    return jax.nn.silu(x)

def _sigmoid(x):
    return jax.nn.sigmoid(x)

def _layernorm(x, axis=-1, eps=1e-05):
    m = jnp.mean(x, axis=axis, keepdims=True)
    v = jnp.var(x, axis=axis, keepdims=True)
    return (x - m) / jnp.sqrt(v + eps)

def _scatter_add(tgt, idx, src, axis=0):
    return tgt.at[idx].add(src)

def _segment_sum(src, seg, n):
    return jax.ops.segment_sum(src, seg, n)
kernel_name = 'mk_gnn_preln_d4_gnn_r8_fdb9a5'

def setup_inputs(seed: int=0):
    np.random.seed(seed)
    _w = jnp.asarray

    def _rec_inputs():
        import jax
        import jax.numpy as jnp
        _gk = jax.random.key(seed)
        x = -0.0003713 + 1 * jax.random.normal(jax.random.fold_in(_gk, 1), (12500, 128), jnp.float32)
        _s = jax.random.randint(jax.random.fold_in(_gk, 2), (100000,), 0, 12500, jnp.int32)
        _d = jax.random.randint(jax.random.fold_in(_gk, 3), (100000,), 0, 12500, jnp.int32)
        _loop = jnp.arange(12500, dtype=jnp.int32)
        src = jnp.concatenate([_s, _d, _loop])
        dst = jnp.concatenate([_d, _s, _loop])
        _o = jnp.argsort(dst, stable=True)
        src = src[_o]
        dst = dst[_o]
        edge_type_16 = jax.random.randint(jax.random.fold_in(_gk, 12), (212500,), 0, 16, jnp.int32)
        edge_type_8 = jax.random.randint(jax.random.fold_in(_gk, 13), (212500,), 0, 8, jnp.int32)
        return (x, src, dst, edge_type_16, edge_type_8)
    x, src, dst, edge_type_16, edge_type_8 = _rec_inputs()

    def _L0_gnn_setup():
        import jax, jax.numpy as jnp
        import numpy as np
        N_NODES = 12500
        N_EDGES = 75000
        HID = 128
        N_ETYPES = 8
        key = jax.random.key(seed)
        ks = jax.random.split(key, 10)
        s = 1.0 / np.sqrt(HID)
        return {'h': jax.random.normal(ks[0], (N_NODES, HID), dtype=jnp.float32), 'edge_index': jax.random.randint(ks[1], (2, N_EDGES), 0, N_NODES, dtype=jnp.int64), 'edge_type': jax.random.randint(ks[2], (N_EDGES,), 0, N_ETYPES, dtype=jnp.int64), 'message_W': jax.random.uniform(ks[3], (N_ETYPES, HID, HID), jnp.float32, -s, s), 'message_b': jax.random.uniform(ks[4], (N_ETYPES, HID), jnp.float32, -s, s), 'gru_w_ih': jax.random.uniform(ks[5], (3 * HID, HID), jnp.float32, -s, s), 'gru_w_hh': jax.random.uniform(ks[6], (3 * HID, HID), jnp.float32, -s, s), 'gru_b_ih': jax.random.uniform(ks[7], (3 * HID,), jnp.float32, -s, s), 'gru_b_hh': jax.random.uniform(ks[8], (3 * HID,), jnp.float32, -s, s)}
    _L0_gnn_all = _L0_gnn_setup()
    _L0_gnn_in = {k: v for k, v in _L0_gnn_all.items() if k in ('message_W', 'message_b', 'gru_w_ih', 'gru_w_hh', 'gru_b_ih', 'gru_b_hh')}
    del _L0_gnn_all

    def _L1_gnn_setup():
        import jax, jax.numpy as jnp
        import numpy as np
        NUM_NODES = 1250
        key = jax.random.key(seed)
        k1, k2, k3, k4 = jax.random.split(key, 4)
        x = jax.random.normal(k1, (NUM_NODES, 128), dtype=jnp.float32)
        edge_index = jax.random.randint(k2, (2, 80000), 0, NUM_NODES, dtype=jnp.int64)
        W = jax.random.normal(k3, (128, 128), dtype=jnp.float32) * (1.0 / np.sqrt(128))
        b = jax.random.normal(k4, (128,), dtype=jnp.float32) * 0.01
        return {'x': x, 'edge_index': edge_index, 'W': W, 'b': b}
    _L1_gnn_all = _L1_gnn_setup()
    _L1_gnn_in = {k: v for k, v in _L1_gnn_all.items() if k in ('W', 'b')}
    del _L1_gnn_all

    def _L2_gnn_setup():
        import jax, jax.numpy as jnp
        import numpy as np
        NUM_NODES = 12500
        NUM_EDGES = 80000
        IN_DIM = 128
        OUT_DIM = 128
        NUM_REL = 16
        key = jax.random.key(seed)
        k1, k2, k3, k4, k5 = jax.random.split(key, 5)
        x = jax.random.normal(k1, (NUM_NODES, IN_DIM), dtype=jnp.float32)
        edge_index = jax.random.randint(k2, (2, NUM_EDGES), 0, NUM_NODES, dtype=jnp.int64)
        edge_types = jax.random.randint(k3, (NUM_EDGES,), 0, NUM_REL, dtype=jnp.int64)
        rw_bound = float(np.sqrt(6.0 / (IN_DIM * OUT_DIM + NUM_REL)))
        relation_weights = jax.random.uniform(k4, (NUM_REL, IN_DIM, OUT_DIM), dtype=jnp.float32, minval=-rw_bound, maxval=rw_bound)
        sw_bound = float(np.sqrt(6.0 / (IN_DIM + OUT_DIM)))
        self_weight = jax.random.uniform(k5, (IN_DIM, OUT_DIM), dtype=jnp.float32, minval=-sw_bound, maxval=sw_bound)
        bias = jnp.zeros((OUT_DIM,), dtype=jnp.float32)
        return {'x': x, 'edge_index': edge_index, 'edge_types': edge_types, 'relation_weights': relation_weights, 'self_weight': self_weight, 'bias': bias}
    _L2_gnn_all = _L2_gnn_setup()
    _L2_gnn_in = {k: v for k, v in _L2_gnn_all.items() if k in ('relation_weights', 'self_weight', 'bias')}
    del _L2_gnn_all

    def _L3_gnn_setup():
        import jax, jax.numpy as jnp
        import numpy as np
        N_NODES = 6250
        N_EDGES = 100000
        IN_DIM = 128
        ADD = 8
        HIDDEN = 256
        OUT_DIM = 128

        def gcn_conv(x, src, dst, W, b, n_nodes):
            loop = jnp.arange(n_nodes, dtype=src.dtype)
            s = jnp.concatenate([src, loop])
            d = jnp.concatenate([dst, loop])
            deg = jax.ops.segment_sum(jnp.ones(s.shape[0], dtype=x.dtype), d, num_segments=n_nodes)
            dinv = jnp.where(deg > 0, jax.lax.rsqrt(deg), 0.0)
            norm = dinv[s] * dinv[d]
            h = x @ W
            msg = h[s] * norm[:, None]
            out = jax.ops.segment_sum(msg, d, num_segments=n_nodes)
            return out + b

        def prelu(x, a):
            return jnp.where(x >= 0, x, a * x)
        key = jax.random.key(seed)
        ks = jax.random.split(key, 8)
        x = jax.random.normal(ks[0], (N_NODES, IN_DIM), dtype=jnp.float32)
        edge_index = jax.random.randint(ks[1], (2, N_EDGES), 0, N_NODES, dtype=jnp.int64)
        id_vec = jax.random.normal(ks[2], (ADD,), dtype=jnp.float32)
        W1 = jax.random.normal(ks[3], (IN_DIM + ADD, HIDDEN), dtype=jnp.float32) * 0.05
        b1 = jnp.zeros((HIDDEN,), dtype=jnp.float32)
        a1 = jnp.full((HIDDEN,), 0.25, dtype=jnp.float32)
        W2 = jax.random.normal(ks[4], (HIDDEN, OUT_DIM), dtype=jnp.float32) * 0.05
        b2 = jnp.zeros((OUT_DIM,), dtype=jnp.float32)
        a2 = jnp.full((OUT_DIM,), 0.25, dtype=jnp.float32)
        return {'x': x, 'edge_index': edge_index, 'id': id_vec, 'W1': W1, 'b1': b1, 'a1': a1, 'W2': W2, 'b2': b2, 'a2': a2}
    _L3_gnn_all = _L3_gnn_setup()
    _L3_gnn_in = {k: v for k, v in _L3_gnn_all.items() if k in ('id', 'W1', 'b1', 'a1', 'W2', 'b2', 'a2')}
    del _L3_gnn_all
    return {'x': x, 'src': src, 'dst': dst, 'edge_type_16': edge_type_16, 'edge_type_8': edge_type_8, 'L0_gnn_message_W': _L0_gnn_in['message_W'], 'L0_gnn_message_b': _L0_gnn_in['message_b'], 'L0_gnn_gru_w_ih': _L0_gnn_in['gru_w_ih'], 'L0_gnn_gru_w_hh': _L0_gnn_in['gru_w_hh'], 'L0_gnn_gru_b_ih': _L0_gnn_in['gru_b_ih'], 'L0_gnn_gru_b_hh': _L0_gnn_in['gru_b_hh'], 'L1_gnn_W': _L1_gnn_in['W'], 'L1_gnn_b': _L1_gnn_in['b'], 'L2_gnn_relation_weights': _L2_gnn_in['relation_weights'], 'L2_gnn_self_weight': _L2_gnn_in['self_weight'], 'L2_gnn_bias': _L2_gnn_in['bias'], 'L3_gnn_id': _L3_gnn_in['id'], 'L3_gnn_W1': _L3_gnn_in['W1'], 'L3_gnn_b1': _L3_gnn_in['b1'], 'L3_gnn_a1': _L3_gnn_in['a1'], 'L3_gnn_W2': _L3_gnn_in['W2'], 'L3_gnn_b2': _L3_gnn_in['b2'], 'L3_gnn_a2': _L3_gnn_in['a2']}

def reference(x, src, dst, edge_type_16, edge_type_8, L0_gnn_message_W, L0_gnn_message_b, L0_gnn_gru_w_ih, L0_gnn_gru_w_hh, L0_gnn_gru_b_ih, L0_gnn_gru_b_hh, L1_gnn_W, L1_gnn_b, L2_gnn_relation_weights, L2_gnn_self_weight, L2_gnn_bias, L3_gnn_id, L3_gnn_W1, L3_gnn_b1, L3_gnn_a1, L3_gnn_W2, L3_gnn_b2, L3_gnn_a2):
    import jax
    import jax.numpy as jnp

    def _L0_gnn_ref(h, edge_index, edge_type, message_W, message_b, gru_w_ih, gru_w_hh, gru_b_ih, gru_b_hh):
        import jax, jax.numpy as jnp
        import numpy as np
        N_NODES = 12500
        N_EDGES = 75000
        HID = 128
        N_ETYPES = 8
        num_nodes = h.shape[0]
        src, dst = (edge_index[0], edge_index[1])
        all_msgs = jnp.einsum('nh,thd->ntd', h, message_W) + message_b
        msg = all_msgs[src, edge_type]
        messages = jax.ops.segment_sum(msg, dst, num_segments=num_nodes)
        gi = messages @ gru_w_ih.T + gru_b_ih
        gh = h @ gru_w_hh.T + gru_b_hh
        i_r, i_z, i_n = jnp.split(gi, 3, axis=-1)
        h_r, h_z, h_n = jnp.split(gh, 3, axis=-1)
        r = jax.nn.sigmoid(i_r + h_r)
        z = jax.nn.sigmoid(i_z + h_z)
        n = jnp.tanh(i_n + r * h_n)
        return (1.0 - z) * n + z * h

    def _L1_gnn_ref(x, edge_index, W, b):
        import jax, jax.numpy as jnp
        import numpy as np
        NUM_NODES = 1250
        src, dst = (edge_index[0], edge_index[1])
        num_nodes = x.shape[0]
        aggregated = jax.ops.segment_sum(x[src], dst, num_segments=num_nodes)
        degree = jax.ops.segment_sum(jnp.ones_like(dst, dtype=x.dtype), dst, num_segments=num_nodes)
        degree = jnp.maximum(degree, 1.0)
        aggregated = aggregated / degree[:, None]
        out = jax.nn.relu(jnp.einsum('nd,od->no', aggregated + x, W) + b)
        return out

    def _L2_gnn_ref(x, edge_index, edge_types, relation_weights, self_weight, bias):
        import jax, jax.numpy as jnp
        import numpy as np
        NUM_NODES = 12500
        NUM_EDGES = 80000
        IN_DIM = 128
        OUT_DIM = 128
        NUM_REL = 16
        num_nodes = x.shape[0]
        self_msg = x @ self_weight
        transformed = jnp.einsum('ni,rio->rno', x, relation_weights)
        src = edge_index[0]
        dst = edge_index[1]
        msgs = transformed[edge_types, src]
        neighbor_msg = jax.ops.segment_sum(msgs, dst, num_segments=num_nodes)
        return jax.nn.relu(self_msg + neighbor_msg + bias)

    def _L3_gnn_ref(x, edge_index, id, W1, b1, a1, W2, b2, a2):
        import jax, jax.numpy as jnp
        import numpy as np
        N_NODES = 6250
        N_EDGES = 100000
        IN_DIM = 128
        ADD = 8
        HIDDEN = 256
        OUT_DIM = 128

        def gcn_conv(x, src, dst, W, b, n_nodes):
            loop = jnp.arange(n_nodes, dtype=src.dtype)
            s = jnp.concatenate([src, loop])
            d = jnp.concatenate([dst, loop])
            deg = jax.ops.segment_sum(jnp.ones(s.shape[0], dtype=x.dtype), d, num_segments=n_nodes)
            dinv = jnp.where(deg > 0, jax.lax.rsqrt(deg), 0.0)
            norm = dinv[s] * dinv[d]
            h = x @ W
            msg = h[s] * norm[:, None]
            out = jax.ops.segment_sum(msg, d, num_segments=n_nodes)
            return out + b

        def prelu(x, a):
            return jnp.where(x >= 0, x, a * x)
        n = x.shape[0]
        src, dst = (edge_index[0], edge_index[1])
        xi = jnp.concatenate([x, jnp.broadcast_to(id[None, :], (n, id.shape[0]))], axis=1)
        h = gcn_conv(xi, src, dst, W1, b1, n)
        h = prelu(h, a1)
        h = gcn_conv(h, src, dst, W2, b2, n)
        h = prelu(h, a2)
        return h
    edge_index = jnp.stack([src, dst])
    h = jnp.maximum(_layernorm(x, axis=-1), 0.0)
    x = x + _L0_gnn_ref(h, edge_index, edge_type_8, L0_gnn_message_W, L0_gnn_message_b, L0_gnn_gru_w_ih, L0_gnn_gru_w_hh, L0_gnn_gru_b_ih, L0_gnn_gru_b_hh)
    h = jnp.maximum(_layernorm(x, axis=-1), 0.0)
    x = x + _L1_gnn_ref(h, edge_index, L1_gnn_W, L1_gnn_b)
    h = jnp.maximum(_layernorm(x, axis=-1), 0.0)
    x = x + _L2_gnn_ref(h, edge_index, edge_type_16, L2_gnn_relation_weights, L2_gnn_self_weight, L2_gnn_bias)
    h = jnp.maximum(_layernorm(x, axis=-1), 0.0)
    x = x + _L3_gnn_ref(h, edge_index, L3_gnn_id, L3_gnn_W1, L3_gnn_b1, L3_gnn_a1, L3_gnn_W2, L3_gnn_b2, L3_gnn_a2)
    return x

_drawn_inputs = setup_inputs


def setup_inputs(seed=0):
    import zlib

    import numpy as np

    out = dict(_drawn_inputs(seed))
    spreads = {'L2_gnn_bias': (0.0, 0.1),
     'L3_gnn_b1': (0.0, 0.408),
     'L3_gnn_a1': (0.25, 0.6),
     'L3_gnn_b2': (0.0, 0.1),
     'L3_gnn_a2': (0.25, 0.6)}
    factors = {'L0_gnn_gru_b_ih': 4.365, 'L0_gnn_gru_b_hh': 5.744, 'L1_gnn_b': 8.0, 'L3_gnn_id': 3.033}
    for name, (base, spread) in spreads.items():
        noise = np.random.default_rng([zlib.crc32(name.encode()), seed]).standard_normal(out[name].shape)
        drawn = base * np.exp(spread * noise) if base else spread * noise
        out[name] = jnp.asarray(drawn.astype(out[name].dtype))
    for name, factor in factors.items():
        out[name] = (out[name] * factor).astype(out[name].dtype)
    return out
```

```python
import concourse.bass as bass
from concourse import mybir
from contextlib import ExitStack

P = 128
F = 128
NODES = 12500
EDGES = 212500
TILES = -(-NODES // P)
NP = TILES * P
CH = 17
STEPS = -(-EDGES // (CH * P))
W = 160
ACC = NP + W
T8, T16 = 8, 16
ROW3 = 132
HID = 256
LAG = 2
EPS = 1e-5
assert STEPS == TILES and TILES % 2 == 0


def gnn_layers(nc, x_in, src, dst, type8, type16, w_msg, b_msg, w_ih, w_hh, b_ih, b_hh, w_l1, b_l1,
               w_rel, w_self, b_l2, id_vec, w1, b1, a1, w2, b2, a2, out):
    f32, i32 = mybir.dt.float32, mybir.dt.int32
    ALU, ACT = mybir.AluOpType, mybir.ActivationFunctionType
    ds = bass.ds

    def scratch(name, shape):
        return nc.dram_tensor(name, shape, f32, kind="Internal").ap()

    tab0 = scratch("table_typed8", (NP * T8, F))
    tab2 = scratch("table_typed16", (NP * T16, F))
    tab3 = scratch("table_scaled", (NP, ROW3))
    tab4 = scratch("table_conv2", (NP, F))
    h0_d, h1_d, h2_d = (scratch(f"h{n}_rows", (NP, F)) for n in range(3))
    x1_d, x2_d, x3_d = (scratch(f"x{n}_rows", (NP, F)) for n in (1, 2, 3))
    deg_d = scratch("degree", (TILES, P))

    ctx = ExitStack()
    with ctx:
        def sb(name, shape, dt=f32):
            return ctx.enter_context(nc.sbuf_tensor(name, shape, dt))

        def pb(name, shape):
            return ctx.enter_context(nc.psum_tensor(name, shape, f32))

        ORDER = ["W", "D", "T", 0, 1, 2, 3, 4]
        ONCE = ("W", "D")
        GIVEN = {
            "h_ready": ("T", 0, 1, 2, 3), "h_transposed": ("T", 0, 1, 2, 3), "hT_ready": ("T", 0, 1, 2),
            "products": ("T", 0, 1, 2, 3, 4), "rows_ready": ("T", 1),
            "stats": ("T", 0, 1, 2), "mean_var": ("T", 0, 1, 2), "rstd": ("T", 0, 1, 2), "std": ("T", 0, 1, 2),
            "norm_ready": ("T", 0, 1, 2), "rstd_scaled": (2,),
            "slot_ready": (0, 1, 2, 3, 4), "hot_ready": (0, 1, 2, 3, 4), "sums_ready": (0, 1, 2, 3, 4),
            "sums_added": (0, 1, 2, 3, 4), "gather_go": (0, 1, 2, 3, 4), "window_ready": (0, 3),
            "aux_added": (0, 3), "acc_zeroed": (0, 1, 2, 3, 4), "aT_ready": (0, 1, 2, 3, 4),
            "x_ready": (0, 1, 2, 4), "dinv_set": (2,),
            "rz_ready": (0,), "cand_in": (0,), "cand_ready": (0,), "r_hn": (0,), "h_less_n": (0,),
            "z_part": (0,), "gru_out": (0,),
            "mean": (1,), "mean_h": (1,), "h2_transposed": (1,), "h2T_ready": (1,), "rows_half": (1,),
            "rows_all": (1,), "rows_ready_act": (1,),
            "hid_ready": (3, 4), "conv_out": (3, 4), "below": (3, 4), "own_loop": (4,),
            "hid_transposed": (3,), "pT_ready": (3,), "products2": (3,),
        }
        SLOTS = {
            "x_loaded": {"T": 1}, "in_loaded": {0: 2, 1: 2, 2: 2, 3: 1, 4: 2},
            "h_stored": {"T": 1, 0: 1, 1: 1, 2: 1, 3: 1}, "x_stored": {0: 1, 1: 1, 2: 1, 4: 1},
            "rows_stored": {"T": 1, 1: 1},
        }
        made = {}

        def total(phase, name):
            if name == "done":
                return 1
            if name in GIVEN:
                return TILES if phase in GIVEN[name] else 0
            return 16 * SLOTS[name[:-1]].get(phase, 0) * (TILES // 2)

        def S(phase, name):
            own = phase in ONCE or name[:-1] == "rows_in"
            key = (phase, name) if own else name
            if key not in made:
                made[key] = ctx.enter_context(nc.semaphore(f"{phase}_{name}" if own else name))
            return made[key]

        def at(phase, name, value):
            if phase in ONCE or name[:-1] == "rows_in" or (isinstance(value, int) and value < 1):
                return S(phase, name), value
            return S(phase, name), sum(total(q, name) for q in ORDER[2:ORDER.index(phase)]) + value

        def after(eng, sem, value):
            if isinstance(value, int) and value < 1:
                return
            eng.wait_ge(sem, value)

        def hold(eng, name):
            eng.sem_inc(S("W", f"{name}_held"), 1)

        acc = sb("acc", [P, ACC])
        aux = sb("aux", [1, ACC])
        src_sb = sb("src_sb", [P, STEPS * CH], i32)
        dst_sb = sb("dst_sb", [P, STEPS * CH], i32)
        typed = sb("typed", [P, STEPS * CH], i32)
        rel = dst_sb[:, :].bitcast(f32)
        base_i = sb("base_i", [1, STEPS], i32)
        slot = [sb(f"slot{k}", [P, CH], i32) for k in range(2)]
        rows = [sb(f"rows{k}", [P, CH, ROW3]) for k in range(2)]
        hot = [sb(f"hot{k}", [P, CH, W]) for k in range(2)]
        node_i = sb("node_i", [P, W], i32)
        node = sb("node", [P, W])
        ident = sb("ident", [P, P])
        ones = sb("ones", [P, P])
        zero = sb("zero", [P, P])
        base_f = sb("base_f", [1, STEPS])
        wih_sb = sb("wih_sb", [P, 3 * F])
        whh_sb = sb("whh_sb", [P, 3 * F])
        bg_sb = sb("bg_sb", [1, 4 * F])
        bh_sb = sb("bh_sb", [1, 2 * F])
        wl1_sb = sb("wl1_sb", [P, F])
        bl1_sb = sb("bl1_sb", [1, F])
        wrel_sb = sb("wrel_sb", [P, T16 * F])
        wself_sb = sb("wself_sb", [P, F])
        bl2_sb = sb("bl2_sb", [1, F])
        id_sb = sb("id_sb", [8, 1])
        w1b_sb = sb("w1b_sb", [8, HID])
        idw_sb = sb("idw_sb", [1, HID])
        deg_t = sb("deg_t", [TILES, P])
        rdeg = sb("rdeg", [P, TILES])
        dinv = sb("dinv", [P, TILES])
        degm = sb("degm", [P, TILES])
        root = sb("root", [P, TILES])
        x_t = [sb(f"x_t{k}", [P, F]) for k in range(2)]
        h_t = [sb(f"h_t{k}", [P, ROW3]) for k in range(2)]
        xo_t = [sb(f"xo_t{k}", [P, F]) for k in range(2)]
        ho_t = [sb(f"ho_t{k}", [P, ROW3]) for k in range(2)]
        big_t = [sb(f"big_t{k}", [P, T16 * F]) for k in range(2)]
        wmsg_sb, bmsg_sb = big_t[0][:, T8 * F:2 * T8 * F], big_t[1][:, T8 * F:2 * T8 * F]
        w1a_sb, b1_sb, a1_sb = (big_t[1][:, n * HID:(n + 1) * HID] for n in range(3))
        w2_sb = big_t[1][:, 3 * HID:4 * HID].rearrange("p (k f) -> p k f", k=2)
        b2_sb, a2_sb = (big_t[1][:, 4 * HID + n * F:4 * HID + (n + 1) * F] for n in range(2))
        hid_a, hid_b, hid_c, pT = (big_t[0][:, n * HID:(n + 1) * HID] for n in range(4))
        hT = [sb(f"hT{k}", [P, P]) for k in range(2)]
        h2T = sb("h2T", [P, P])
        aT = sb("aT", [P, P])
        aux_t = sb("aux_t", [1, P])
        rz = sb("rz", [P, 2 * F])
        gate_a, gate_b, cand = (sb(n, [P, F]) for n in ("gate_a", "gate_b", "cand"))
        stats = [sb(f"stats{k}", [P, 6]) for k in range(2)]
        mv = [sb(f"mv{k}", [P, 2]) for k in range(2)]
        std = [sb(f"std{k}", [P, 1]) for k in range(2)]
        eps = sb("eps", [P, 1])
        rstd = [sb(f"rstd{k}", [P, 1]) for k in range(2)]
        nmr = [sb(f"nmr{k}", [P, 1]) for k in range(2)]

        big = pb("big", [P, 4 * 512])
        win = [pb(f"win{k}", [P, 512]) for k in range(2)]
        auxp = pb("auxp", [P, 512])
        trp = pb("trp", [P, 512])

        TABLE = [tab0, h1_d, tab2, tab3, tab4]
        INDEX = [typed, src_sb, typed, src_sb, src_sb]
        WIDTH = [F, F, F, ROW3, F]
        X_IN = [x_in, x1_d, x2_d, None, x3_d]
        H_IN = [h0_d, h1_d, h2_d, tab3, tab4]
        X_OUT = [x1_d, x2_d, x3_d, None, out]
        H_OUT = [h1_d, h2_d, tab3, tab4, None]
        AUX = (0, 3)

        def steps(eng, p, agg, dense):
            for t in range(4):
                dense_first(p, t - LAG, dense)
                agg(t, t // 2, t % 2)
            with eng.Fori(2, STEPS // 2) as i:
                for k in range(2):
                    dense(2 * i + k - LAG, i - 1, k)
                    agg(2 * i + k, i, k)

        def steps_agg_first(eng, agg, dense):
            for t in range(4):
                agg(t, t // 2, t % 2)
                if t >= LAG:
                    dense(t - LAG, (t - LAG) // 2, t % 2)
            with eng.Fori(2, STEPS // 2) as i:
                for k in range(2):
                    agg(2 * i + k, i, k)
                    dense(2 * i + k - LAG, i - 1, k)

        def dense_first(p, t, dense):
            if t >= 0:
                dense(t, t // 2, t % 2)

        def last(dense):
            for t in range(TILES - LAG, TILES):
                dense(t, t // 2, t % 2)

        def tile_rows(ap, t):
            return ap[ds(t * P, P), :]

        def typed_rows(ap, t, n):
            return ap[ds(t * (P * n), P * n), :].rearrange("(p r) f -> p (r f)", r=n)

        block = ctx.enter_context(nc.Block())

        @block.sync
        def _(sp):
            def load_first(t, k):
                sp.dma_start(x_t[k][:, :], tile_rows(x_in, t)).then_inc(S("T", f"x_loaded{k}"), 16)

            def store_h(t, i, k):
                sp.wait_ge(*at("T", "h_ready", t + 1))
                hold(sp, "sp")
                sp.dma_start(tile_rows(h0_d, t), ho_t[k][:, 0:F]).then_inc(S("T", f"h_stored{k}"), 16)

            def store_rows(t, i, k):
                sp.wait_ge(*at("T", "rows_ready", t + 1))
                hold(sp, "sp")
                sp.dma_start(typed_rows(tab0, t, T8), big_t[k][:, 0:T8 * F]).then_inc(S("T", f"rows_stored{k}"), 16)

            load_first(0, 0)
            load_first(1, 1)
            sp.dma_start(src_sb[:, :], src).then_inc(S("W", "edges"), 16)
            sp.dma_start(dst_sb[:, :], dst).then_inc(S("W", "edges"), 16)
            sp.dma_start(typed[:, :], type8).then_inc(S("W", "edges"), 16)
            for t in range(2):
                store_h(t, 0, t)
                load_first(t + 2, t)
            with sp.Fori(1, TILES // 2 - 1) as i:
                for k in range(2):
                    store_h(2 * i + k, i, k)
                    load_first(2 * i + k + 2, k)
                    store_rows(2 * i + k - 2, i - 1, k)
            for t in range(TILES - 2, TILES):
                store_h(t, t // 2, t % 2)
                store_rows(t - 2, t // 2 - 1, t % 2)
            for t in range(TILES - 2, TILES):
                store_rows(t, t // 2, t % 2)
            for k in range(2):
                sp.wait_ge(*at("T", f"h_stored{k}", 16 * (TILES // 2)))
                sp.wait_ge(*at("T", f"rows_stored{k}", 16 * (TILES // 2)))
            sp.sem_inc(S("T", "done"), 1)

            for p in range(5):
                def agg(t, i, k):
                    pass

                def dense(t, i, k, p=p):
                    after(sp, *at(p, "x_ready" if p != 3 else "h_transposed", t - 1))
                    hold(sp, "sp")
                    if X_IN[p] is not None:
                        sp.dma_start(x_t[k][:, :], tile_rows(X_IN[p], t)).then_inc(S(p, f"in_loaded{k}"), 16)
                    hw = H_IN[p].shape[1]
                    sp.dma_start(h_t[k][:, 0:hw], tile_rows(H_IN[p], t)).then_inc(S(p, f"in_loaded{k}"), 16)
                    if X_OUT[p] is not None:
                        sp.wait_ge(*at(p, "x_ready", t + 1))
                        hold(sp, "sp")
                        sp.dma_start(tile_rows(X_OUT[p], t), xo_t[k][:, :]).then_inc(S(p, f"x_stored{k}"), 16)
                    if H_OUT[p] is not None:
                        hw = H_OUT[p].shape[1]
                        sp.wait_ge(*at(p, "h_ready", t + 1))
                        hold(sp, "sp")
                        if p == 2:
                            sp.wait_ge(*at(p, "dinv_set", t + 1))
                            hold(sp, "sp")
                        sp.dma_start(tile_rows(H_OUT[p], t), ho_t[k][:, 0:hw]).then_inc(S(p, f"h_stored{k}"), 16)
                    if p == 1:
                        sp.wait_ge(*at(p, "rows_ready", t + 1))
                        hold(sp, "sp")
                        sp.wait_ge(*at(p, "rows_ready_act", t + 1))
                        hold(sp, "sp")
                        sp.dma_start(typed_rows(tab2, t, T16), big_t[k][:, :]).then_inc(S(p, f"rows_stored{k}"), 16)

                if p == 1:
                    sp.dma_start(typed[:, :], type16).then_inc(S("W", "type16"), 16)
                    sp.dma_start(deg_d.rearrange("(o t) p -> o (t p)", o=1), aux[0:1, 0:NP]).then_inc(S("D", "deg_out"), 16)
                    sp.wait_ge(*at("D", "deg_out", 16))
                    sp.dma_start(deg_t[:, :], deg_d).then_inc(S("D", "deg_in"), 16)
                steps(sp, p, agg, dense)
                last(dense)
                for k in range(2):
                    for name, used in (("x", X_OUT[p] is not None), ("h", H_OUT[p] is not None), ("rows", p == 1)):
                        if used:
                            sp.wait_ge(*at(p, f"{name}_stored{k}", 16 * (TILES // 2)))
                sp.sem_inc(S(p, "done"), 1)

        @block.gpsimd
        def _(pool):
            pool.iota(node_i[:, :], [[1, W]], base=0, channel_multiplier=0).then_inc(S("W", "node_i"), 1)
            pool.memset(zero[:, :], 0.0)
            pool.memset(ones[:, :], 1.0).then_inc(S("W", "ones"), 1)
            pool.memset(eps[:, :], EPS).then_inc(S("W", "eps"), 1)
            pool.memset(ident[:, :], 0.0).then_inc(S("W", "zeroed"), 1)
            pool.wait_ge(*at("W", "zeroed", 1))
            pool.affine_select(out=ident[:, :], in_=ident[:, :], compare_op=ALU.not_equal, fill=1.0, base=0,
                               pattern=[[-1, P]], channel_multiplier=1).then_inc(S("W", "ident"), 1)
            pool.memset(aux[:, :], 0.0)
            pool.memset(acc[:, :], 0.0).then_inc(S("W", "acc_zero"), 1)

            for p in range(5):
                pool.wait_ge(*at("T" if p == 0 else p - 1, "done", 1))
                n = TABLE[p].shape[0]

                def agg(t, i, k, p=p):
                    pool.wait_ge(*at(p, "slot_ready", t + 1))
                    after(pool, *at(p, "sums_ready", t - 1))
                    pool.sem_inc(S(p, "gather_go"), 1)
                    for c in range(CH):
                        pool.indirect_dma_start(
                            rows[k][:, c, 0:WIDTH[p]], None, TABLE[p],
                            bass.IndirectOffsetOnAxis(ap=slot[k][:, c:c + 1], axis=0),
                        ).then_inc(S(p, f"rows_in{k}"), 16)

                steps(pool, p, agg, lambda t, i, k: None)

        @block.scalar
        def _(act):
            def load(dst_ap, src_ap, group):
                act.dma_start(dst_ap, src_ap).then_inc(S("W", group), 16)

            def spread(vec):
                return vec.rearrange("(o n) -> o n", o=1)

            load(wmsg_sb, w_msg, "msg")
            load(bmsg_sb, b_msg.partition_broadcast(P), "msg")
            load(bg_sb[:, 0:3 * F], spread(b_ih), "gru")
            load(bg_sb[:, 3 * F:4 * F], spread(b_hh)[:, 2 * F:3 * F], "gru")
            load(bh_sb[:, :], spread(b_hh)[:, 0:2 * F], "gru")
            load(wih_sb[:, :], w_ih, "gru")
            load(whh_sb[:, :], w_hh, "gru")
            load(wl1_sb[:, :], w_l1, "rest")
            load(bl1_sb[:, :], spread(b_l1), "rest")
            load(wrel_sb[:, :], w_rel, "rest")
            load(wself_sb[:, :], w_self, "rest")
            load(bl2_sb[:, :], spread(b_l2), "rest")
            load(id_sb[:, :], id_vec.rearrange("(n o) -> n o", o=1), "rest")
            load(w1b_sb[:, :], w1[F:F + 8, :], "rest")

            def deviation(ph, t, k):
                act.wait_ge(*at(ph, "mean_var", t + 1))
                act.activation(std[k][:, :], mv[k][:, 1:2], ACT.Sqrt, bias=eps[:, 0:1]).then_inc(S(ph, "std"), 1)

            def normalise(ph, t, k, x_ap, h_ap):
                act.wait_ge(*at(ph, "norm_ready", t + 1))
                act.activation(h_ap, x_ap, ACT.Relu, bias=nmr[k][:, 0:1], scale=rstd[k][:, 0:1]).then_inc(S(ph, "h_ready"), 1)

            def first(t, i, k):
                after(act, *at("T", f"h_stored{k}", 16 * i))
                deviation("T", t, k)
                normalise("T", t, k, x_t[k][:, :], ho_t[k][:, 0:F])
                act.wait_ge(*at("T", "h_transposed", t + 1))
                after(act, *at("T", "products", t - 1))
                act.copy(hT[k][:, :], trp[:, 0:P]).then_inc(S("T", "hT_ready"), 1)

            act.wait_ge(*at("W", "eps", 1))
            for t in range(2):
                first(t, 0, t)
            with act.Fori(1, TILES // 2) as i:
                for k in range(2):
                    first(2 * i + k, i, k)

            for p in range(5):
                def agg(t, i, k, p=p):
                    after(act, *at(p, f"rows_in{k}", 16 * CH * i))
                    act.copy(slot[k][:, :], INDEX[p][:, ds(t * CH, CH)]).then_inc(S(p, "slot_ready"), 1)

                def dense(t, i, k, p=p):
                    if p in (0, 1, 2):
                        act.wait_ge(*at(p, "h_transposed", t + 1))
                        act.copy(hT[0][:, :], trp[:, 0:P]).then_inc(S(p, "hT_ready"), 1)
                    if p == 0:
                        act.wait_ge(*at(p, "products", t + 1))
                        act.activation(rz[:, :], big[:, 0:2 * F], ACT.Sigmoid).then_inc(S(p, "rz_ready"), 1)
                        act.wait_ge(*at(p, "cand_in", t + 1))
                        act.activation(cand[:, :], gate_b[:, :], ACT.Tanh).then_inc(S(p, "cand_ready"), 1)
                    if p in (0, 1, 2):
                        after(act, *at(p, f"h_stored{k}", 16 * i))
                        deviation(p, t, k)
                        normalise(p, t, k, xo_t[k][:, :], ho_t[k][:, 0:F])
                    if p == 1:
                        act.wait_ge(*at(p, "h2_transposed", t + 1))
                        act.copy(h2T[:, :], trp[:, 0:P]).then_inc(S(p, "h2T_ready"), 1)
                        after(act, *at(p, f"rows_stored{k}", 16 * i))
                        act.wait_ge(*at(p, "rows_half", t + 1))
                        act.copy(big_t[k][:, 0:8 * F], big[:, 0:8 * F]).then_inc(S(p, "rows_ready_act"), 1)
                    if p == 3:
                        act.wait_ge(*at(p, "hid_transposed", t + 1))
                        act.copy(pT, trp[:, 0:HID]).then_inc(S(p, "pT_ready"), 1)
                        act.wait_ge(*at(p, "products2", t + 1))
                        after(act, *at(p, f"h_stored{k}", 16 * i))
                        act.activation(ho_t[k][:, 0:F], big[:, 512:512 + F], ACT.Identity,
                                       scale=dinv[:, ds(t, 1)]).then_inc(S(p, "h_ready"), 1)

                act.wait_ge(*at("T" if p == 0 else p - 1, "done", 1))
                if p == 0:
                    act.wait_ge(*at("W", "idx8", 1))
                if p == 1:
                    act.wait_ge(*at("D", "degm", 1))
                    act.activation(root[:, :], trp[:, 0:TILES], ACT.Sqrt, bias=ones[:, 0:1]).then_inc(S("D", "root"), 1)
                if p == 2:
                    act.wait_ge(*at("W", "idx16", 1))
                    load(w1a_sb, w1[0:F, :], "late")
                    load(b1_sb, b1.partition_broadcast(P), "late")
                    load(a1_sb, a1.partition_broadcast(P), "late")
                    load(w2_sb, w2.rearrange("(k p) f -> p k f", k=2), "late")
                    load(b2_sb, b2.partition_broadcast(P), "late")
                    load(a2_sb, a2.partition_broadcast(P), "late")
                steps_agg_first(act, agg, dense)
                last(dense)

        @block.tensor
        def _(pe):
            mm = nc.tensor.matmul
            pe.wait_ge(*at("W", "ones", 1))
            pe.wait_ge(*at("W", "ident", 1))
            pe.wait_ge(*at("W", "base_f", 1))
            mm(auxp[:, 0:STEPS], ones[0:1, :], base_f[:, :], start=True, stop=True).then_inc(S("W", "base_all"), 1)
            pe.wait_ge(*at("W", "msg", 32))

            def transpose_first(t, i, k):
                pe.wait_ge(*at("T", "h_ready", t + 1))
                after(pe, *at("T", "hT_ready", t))
                nc.tensor.transpose(trp[:, 0:P], ho_t[k][:, 0:F], ident[:, :]).then_inc(S("T", "h_transposed"), 1)

            def products_first(t, i, k):
                pe.wait_ge(*at("T", "hT_ready", t + 1))
                after(pe, *at("T", "rows_ready", t - 1))
                for j in range(2):
                    last_mm = mm(big[:, (2 * k + j) * 512:(2 * k + j + 1) * 512], hT[k][:, :],
                                 wmsg_sb[:, j * 512:(j + 1) * 512], start=True, stop=True)
                last_mm.then_inc(S("T", "products"), 1)

            transpose_first(0, 0, 0)
            transpose_first(1, 0, 1)
            products_first(0, 0, 0)
            with pe.Fori(1, TILES // 2) as i:
                transpose_first(2 * i, i, 0)
                products_first(2 * i - 1, i - 1, 1)
                transpose_first(2 * i + 1, i, 1)
                products_first(2 * i, i, 0)
            products_first(TILES - 1, TILES // 2 - 1, 1)

            pe.wait_ge(*at("W", "gru", 16 * 5))
            pe.wait_ge(*at("W", "bg", 1))
            pe.wait_ge(*at("W", "rest", 16 * 7))
            pe.wait_ge(*at("W", "rel", 1))
            mm(auxp[0:1, 0:HID], id_sb[:, :], w1b_sb[:, :], start=True, stop=True).then_inc(S("W", "idw_mm"), 1)
            pe.wait_ge(*at("W", "idw", 1))

            for p in range(5):
                pe.wait_ge(*at("T" if p == 0 else p - 1, "done", 1))
                if p == 3:
                    pe.wait_ge(*at("W", "late", 16 * 6))
                if p == 1:
                    pe.wait_ge(*at("D", "deg_in", 16))
                    nc.tensor.transpose(trp[:, 0:TILES], deg_t[:, :], ident[0:TILES, 0:TILES]).then_inc(S("D", "deg_cols"), 1)
                    pe.wait_ge(*at("D", "deg_done", 1))

                def agg(t, i, k, p=p):
                    pe.wait_ge(*at(p, f"rows_in{k}", 16 * CH * (i + 1)))
                    pe.wait_ge(*at(p, "hot_ready", t + 1))
                    after(pe, *at(p, "sums_added", t - 1))
                    for c in range(CH):
                        last_mm = mm(win[k][:, 0:W], rows[k][:, c, 0:F], hot[k][:, c, :], start=c == 0, stop=c == CH - 1)
                    if p in AUX:
                        last_mm.then_inc(S(p, "window_ready"), 1)
                        after(pe, *at(p, "aux_added", t))
                        for c in range(CH):
                            one = ones[:, 0:1] if p == 0 else rows[k][:, c, F:F + 1]
                            last_mm = mm(auxp[0:1, 0:W], one, hot[k][:, c, :], start=c == 0, stop=c == CH - 1)
                    last_mm.then_inc(S(p, "sums_ready"), 1)

                def dense(t, i, k, p=p):
                    if p != 4:
                        n_in = 1 if X_IN[p] is None else 2
                        pe.wait_ge(*at(p, f"in_loaded{k}", 16 * n_in * (i + 1)))
                        last_mm = nc.tensor.transpose(trp[:, 0:P], h_t[k][:, 0:F], ident[:, :])
                        if p == 3:
                            last_mm = nc.tensor.transpose(trp[0:1, P:2 * P], h_t[k][:, F:F + 1], ident[:, :])
                        last_mm.then_inc(S(p, "h_transposed"), 1)
                    pe.wait_ge(*at(p, "aT_ready", t + 1))
                    if p == 0:
                        mm(big[:, 0:4 * F], ones[0:1, :], bg_sb[:, :], start=True, stop=False)
                        mm(big[:, 0:3 * F], aT[:, :], wih_sb[:, :], start=False, stop=False)
                        pe.wait_ge(*at(p, "hT_ready", t + 1))
                        mm(big[:, 0:2 * F], hT[0][:, :], whh_sb[:, 0:2 * F], start=False, stop=False)
                        mm(big[:, 3 * F:4 * F], hT[0][:, :], whh_sb[:, 2 * F:3 * F], start=False, stop=True)\
                            .then_inc(S(p, "products"), 1)
                    if p == 1:
                        mm(big[:, 0:F], aT[:, :], wl1_sb[:, :], start=True, stop=True)
                        mm(big[:, 512:512 + F], ones[0:1, :], bl1_sb[:, :], start=True, stop=False)
                        pe.wait_ge(*at(p, "hT_ready", t + 1))
                        mm(big[:, 512:512 + F], hT[0][:, :], wl1_sb[:, :], start=False, stop=True)\
                            .then_inc(S(p, "products"), 1)
                        pe.wait_ge(*at(p, "h_ready", t + 1))
                        nc.tensor.transpose(trp[:, 0:P], ho_t[k][:, 0:F], ident[:, :]).then_inc(S(p, "h2_transposed"), 1)
                        pe.wait_ge(*at(p, "h2T_ready", t + 1))
                        for j in range(4):
                            last_mm = mm(big[:, j * 512:(j + 1) * 512], h2T[:, :], wrel_sb[:, j * 512:(j + 1) * 512],
                                         start=True, stop=True)
                            if j == 1:
                                last_mm.then_inc(S(p, "rows_half"), 1)
                        last_mm.then_inc(S(p, "rows_all"), 1)
                    if p == 2:
                        mm(big[:, 0:F], ones[0:1, :], bl2_sb[:, :], start=True, stop=False)
                        mm(big[:, 0:F], aT[:, :], ident[:, :], start=False, stop=False)
                        pe.wait_ge(*at(p, "hT_ready", t + 1))
                        mm(big[:, 0:F], hT[0][:, :], wself_sb[:, :], start=False, stop=True).then_inc(S(p, "products"), 1)
                    if p == 3:
                        mm(big[:, 0:HID], aT[:, :], w1a_sb, start=True, stop=False)
                        mm(big[:, 0:HID], aux_t[:, :], idw_sb[:, :], start=False, stop=True).then_inc(S(p, "products"), 1)
                        pe.wait_ge(*at(p, "hid_ready", t + 1))
                        for j in range(2):
                            last_mm = nc.tensor.transpose(trp[:, j * P:(j + 1) * P], hid_c[:, j * P:(j + 1) * P], ident[:, :])
                        last_mm.then_inc(S(p, "hid_transposed"), 1)
                        pe.wait_ge(*at(p, "pT_ready", t + 1))
                        for j in range(2):
                            last_mm = mm(big[:, 512:512 + F], pT[:, j * P:(j + 1) * P], w2_sb[:, j, :],
                                         start=j == 0, stop=j == 1)
                        last_mm.then_inc(S(p, "products2"), 1)
                    if p == 4:
                        nc.tensor.transpose(big[:, 0:F], aT[:, :], ident[:, :]).then_inc(S(p, "products"), 1)

                steps(pe, p, agg, dense)
                last(dense)

        @block.vector
        def _(dve):
            V = nc.vector
            dve.wait_ge(*at("W", "node_i", 1))
            V.tensor_copy(node[:, :], node_i[:, :]).then_inc(S("W", "node"), 1)

            def moments(ph, t, k, x_ap):
                V.bn_stats(stats[k][:, :], x_ap).then_inc(S(ph, "stats"), 1)
                dve.wait_ge(*at(ph, "stats", t + 1))
                hold(dve, "dve")
                V.bn_aggr(mv[k][:, :], stats[k][:, :]).then_inc(S(ph, "mean_var"), 1)

            def normalise(ph, t, k, scale=None):
                dve.wait_ge(*at(ph, "std", t + 1))
                V.reciprocal(rstd[k][:, :], std[k][:, :]).then_inc(S(ph, "rstd"), 1)
                dve.wait_ge(*at(ph, "rstd", t + 1))
                if scale is not None:
                    V.tensor_scalar(rstd[k][:, :], rstd[k][:, :], scale, None, ALU.mult).then_inc(S(ph, "rstd_scaled"), 1)
                    dve.wait_ge(*at(ph, "rstd_scaled", t + 1))
                V.scalar_tensor_tensor(out=nmr[k][:, :], in0=mv[k][:, 0:1], scalar=-1.0, in1=rstd[k][:, :],
                                       op0=ALU.mult, op1=ALU.mult).then_inc(S(ph, "norm_ready"), 1)

            def moments_first(t, i, k):
                dve.wait_ge(*at("T", f"x_loaded{k}", 16 * (i + 1)))
                after(dve, *at("T", "h_ready", t - 1))
                moments("T", t, k, x_t[k][:, :])

            def rows_first(t, i, k):
                dve.wait_ge(*at("T", "products", t + 1))
                after(dve, *at("T", f"rows_stored{k}", 16 * i))
                V.tensor_tensor(big_t[k][:, 0:T8 * F], big[:, k * 1024:(k + 1) * 1024], bmsg_sb, ALU.add)\
                    .then_inc(S("T", "rows_ready"), 1)

            dve.wait_ge(*at("W", "edges", 48))
            V.tensor_copy(base_i[:, :], dst_sb[0:1, :].rearrange("o (s c) -> o s c", c=CH)[:, :, 0])
            V.tensor_copy(base_f[:, :], dst_sb[0:1, :].rearrange("o (s c) -> o s c", c=CH)[:, :, 0]).then_inc(S("W", "base_f"), 1)
            V.scalar_tensor_tensor(out=typed[:, :], in0=src_sb[:, :], scalar=float(T8), in1=typed[:, :],
                                   op0=ALU.mult, op1=ALU.add).then_inc(S("W", "idx8"), 1)
            dve.wait_ge(*at("W", "base_all", 1))
            V.tensor_tensor(rel.rearrange("p (s c) -> p s c", c=CH), dst_sb[:, :].rearrange("p (s c) -> p s c", c=CH),
                            auxp[:, 0:STEPS].unsqueeze(2).to_broadcast([P, STEPS, CH]), ALU.subtract).then_inc(S("W", "rel"), 1)
            dve.wait_ge(*at("W", "gru", 16 * 5))
            V.tensor_tensor(bg_sb[:, 0:2 * F], bg_sb[:, 0:2 * F], bh_sb[:, :], ALU.add).then_inc(S("W", "bg"), 1)
            for t in range(2):
                moments_first(t, 0, t)
                normalise("T", t, t)
            dve.wait_ge(*at("W", "msg", 32))
            for t in range(2, 4):
                moments_first(t, t // 2, t % 2)
                rows_first(t - 2, t // 2 - 1, t % 2)
                normalise("T", t, t % 2)
            with dve.Fori(2, TILES // 2) as i:
                for k in range(2):
                    moments_first(2 * i + k, i, k)
                    rows_first(2 * i + k - 2, i - 1, k)
                    normalise("T", 2 * i + k, k)
            for t in range(TILES - 2, TILES):
                rows_first(t, t // 2, t % 2)
            dve.wait_ge(*at("W", "idw_mm", 1))
            V.tensor_copy(idw_sb[:, :], auxp[0:1, 0:HID]).then_inc(S("W", "idw"), 1)
            dve.wait_ge(*at("W", "node", 1))
            dve.wait_ge(*at("W", "acc_zero", 1))
            dve.wait_ge(*at("W", "rest", 16 * 7))

            for p in range(5):
                dve.wait_ge(*at("T" if p == 0 else p - 1, "done", 1))
                if p == 1:
                    dve.wait_ge(*at("W", "type16", 16))
                    V.scalar_tensor_tensor(out=typed[:, :], in0=src_sb[:, :], scalar=float(T16), in1=typed[:, :],
                                           op0=ALU.mult, op1=ALU.add).then_inc(S("W", "idx16"), 1)
                    dve.wait_ge(*at("D", "deg_cols", 1))
                    V.tensor_scalar(degm[:, :], trp[:, 0:TILES], 1.0, None, ALU.max).then_inc(S("D", "degm"), 1)
                    dve.wait_ge(*at("D", "root", 1))
                    V.reciprocal(dinv[:, :], root[:, :])
                    dve.wait_ge(*at("D", "degm", 1))
                    V.reciprocal(rdeg[:, :], degm[:, :]).then_inc(S("D", "deg_done"), 1)
                    dve.wait_ge(*at("D", "deg_done", 1))
                if p == 3:
                    dve.wait_ge(*at("W", "late", 16 * 6))
                if p == 2:
                    V.memset(aux[:, :], 0.0).then_inc(S("D", "aux_zero"), 1)
                    dve.wait_ge(*at("D", "aux_zero", 1))

                def agg(t, i, k, p=p):
                    after(dve, *at(p, "sums_ready", t - 1))
                    V.tensor_tensor(hot[k][:, :, :], node[:, :].unsqueeze(1).to_broadcast([P, CH, W]),
                                    rel[:, ds(t * CH, CH)].unsqueeze(2).to_broadcast([P, CH, W]),
                                    ALU.is_equal).then_inc(S(p, "hot_ready"), 1)

                def add(t, i, k, p=p):
                    base = dve.value_load(base_i[0:1, ds(t, 1)], min_val=0, max_val=NP)
                    after(dve, *at(p, "sums_added", t))
                    after(dve, *at(p, "acc_zeroed", t - LAG))
                    dve.wait_ge(*at(p, "window_ready" if p in AUX else "sums_ready", t + 1))
                    V.tensor_tensor(acc[:, ds(base, W)], acc[:, ds(base, W)], win[k][:, 0:W], ALU.add)\
                        .then_inc(S(p, "sums_added"), 1)
                    if p in AUX:
                        after(dve, *at(p, "aux_added", t))
                        dve.wait_ge(*at(p, "sums_ready", t + 1))
                        V.tensor_tensor(aux[:, ds(base, W)], aux[:, ds(base, W)], auxp[0:1, 0:W], ALU.add)\
                            .then_inc(S(p, "aux_added"), 1)

                def dense(t, i, k, p=p):
                    tile_acc = acc[:, ds(t * P, P)]
                    done = t + LAG if t is not None else 0
                    dve.wait_ge(*at(p, "sums_added", done if not isinstance(t, int) else min(done, STEPS)))
                    if p == 3:
                        dve.wait_ge(*at(p, "aux_added", done if not isinstance(t, int) else min(done, STEPS)))
                        dve.wait_ge(*at(p, "h_transposed", t + 1))
                        V.tensor_tensor(aT[:, :], tile_acc, trp[:, 0:P], ALU.add)
                        V.tensor_tensor(aux_t[:, :], aux[:, ds(t * P, P)], trp[0:1, P:2 * P], ALU.add)\
                            .then_inc(S(p, "aT_ready"), 1)
                    else:
                        V.tensor_scalar(aT[:, :], tile_acc, 1.0, None, ALU.mult).then_inc(S(p, "aT_ready"), 1)
                    dve.wait_ge(*at(p, "aT_ready", t + 1))
                    V.tensor_scalar(tile_acc, zero[:, :], 1.0, None, ALU.mult).then_inc(S(p, "acc_zeroed"), 1)
                    n_in = 1 if X_IN[p] is None else 2
                    dve.wait_ge(*at(p, f"in_loaded{k}", 16 * n_in * (i + 1)))
                    if X_OUT[p] is not None:
                        after(dve, *at(p, f"x_stored{k}", 16 * i))
                    if p == 0:
                        dve.wait_ge(*at(p, "rz_ready", t + 1))
                        V.tensor_tensor(gate_a[:, :], rz[:, 0:F], big[:, 3 * F:4 * F], ALU.mult).then_inc(S(p, "r_hn"), 1)
                        dve.wait_ge(*at(p, "r_hn", t + 1))
                        V.tensor_tensor(gate_b[:, :], gate_a[:, :], big[:, 2 * F:3 * F], ALU.add).then_inc(S(p, "cand_in"), 1)
                        dve.wait_ge(*at(p, "cand_ready", t + 1))
                        V.tensor_tensor(gate_a[:, :], h_t[k][:, 0:F], cand[:, :], ALU.subtract).then_inc(S(p, "h_less_n"), 1)
                        dve.wait_ge(*at(p, "h_less_n", t + 1))
                        V.tensor_tensor(gate_b[:, :], rz[:, F:2 * F], gate_a[:, :], ALU.mult).then_inc(S(p, "z_part"), 1)
                        dve.wait_ge(*at(p, "z_part", t + 1))
                        V.tensor_tensor(gate_a[:, :], gate_b[:, :], cand[:, :], ALU.add).then_inc(S(p, "gru_out"), 1)
                        dve.wait_ge(*at(p, "gru_out", t + 1))
                        V.tensor_tensor(xo_t[k][:, :], gate_a[:, :], x_t[k][:, :], ALU.add).then_inc(S(p, "x_ready"), 1)
                    if p == 1:
                        dve.wait_ge(*at(p, "products", t + 1))
                        V.tensor_scalar(gate_a[:, :], big[:, 0:F], rdeg[:, ds(t, 1)], None, ALU.mult).then_inc(S(p, "mean"), 1)
                        dve.wait_ge(*at(p, "mean", t + 1))
                        V.tensor_tensor(gate_b[:, :], gate_a[:, :], big[:, 512:512 + F], ALU.add).then_inc(S(p, "mean_h"), 1)
                        dve.wait_ge(*at(p, "mean_h", t + 1))
                        V.scalar_tensor_tensor(out=xo_t[k][:, :], in0=gate_b[:, :], scalar=0.0, in1=x_t[k][:, :],
                                               op0=ALU.max, op1=ALU.add).then_inc(S(p, "x_ready"), 1)
                    if p == 2:
                        dve.wait_ge(*at(p, "products", t + 1))
                        V.scalar_tensor_tensor(out=xo_t[k][:, :], in0=big[:, 0:F], scalar=0.0, in1=x_t[k][:, :],
                                               op0=ALU.max, op1=ALU.add).then_inc(S(p, "x_ready"), 1)
                    if p in (0, 1, 2):
                        dve.wait_ge(*at(p, "x_ready", t + 1))
                        if p == 2:
                            after(dve, *at(p, f"h_stored{k}", 16 * i))
                            V.tensor_scalar(ho_t[k][:, F:ROW3], ones[:, 0:ROW3 - F], dinv[:, ds(t, 1)], None, ALU.mult)\
                                .then_inc(S(p, "dinv_set"), 1)
                        after(dve, *at(p, "h_ready", t - 1))
                        moments(p, t, k, xo_t[k][:, :])
                        normalise(p, t, k, dinv[:, ds(t, 1)] if p == 2 else None)
                    if p == 1:
                        dve.wait_ge(*at(p, "rows_all", t + 1))
                        after(dve, *at(p, f"rows_stored{k}", 16 * i))
                        V.tensor_copy(big_t[k][:, 8 * F:], big[:, 8 * F:]).then_inc(S(p, "rows_ready"), 1)
                    if p in (3, 4):
                        n, o, b_sb, a_sb = (HID, "dinv_b", b1_sb, a1_sb) if p == 3 else (F, "dinv_b", b2_sb, a2_sb)
                        dve.wait_ge(*at(p, "products", t + 1))
                        pre = big[:, 0:n]
                        if p == 4:
                            V.tensor_tensor(hid_b[:, 0:n], big[:, 0:n], h_t[k][:, 0:F], ALU.add).then_inc(S(p, "own_loop"), 1)
                            dve.wait_ge(*at(p, "own_loop", t + 1))
                            pre = hid_b[:, 0:n]
                        V.scalar_tensor_tensor(out=hid_a[:, 0:n], in0=pre, scalar=dinv[:, ds(t, 1)], in1=b_sb,
                                               op0=ALU.mult, op1=ALU.add).then_inc(S(p, "conv_out"), 1)
                        dve.wait_ge(*at(p, "conv_out", t + 1))
                        V.scalar_tensor_tensor(out=hid_b[:, 0:n], in0=hid_a[:, 0:n], scalar=0.0, in1=a_sb,
                                               op0=ALU.min, op1=ALU.mult).then_inc(S(p, "below"), 1)
                        dve.wait_ge(*at(p, "below", t + 1))
                        V.scalar_tensor_tensor(out=hid_c[:, 0:n], in0=hid_a[:, 0:n], scalar=0.0, in1=hid_b[:, 0:n],
                                               op0=ALU.max, op1=ALU.add).then_inc(S(p, "hid_ready"), 1)
                    if p == 4:
                        dve.wait_ge(*at(p, "hid_ready", t + 1))
                        V.tensor_tensor(xo_t[k][:, :], hid_c[:, 0:F], x_t[k][:, :], ALU.add).then_inc(S(p, "x_ready"), 1)

                def add_before(t, agg=agg, add=add):
                    pass

                agg(0, 0, 0)
                for t in range(1, 4):
                    agg(t, t // 2, t % 2)
                    add(t - 1, (t - 1) // 2, (t - 1) % 2)
                    if t >= LAG:
                        dense(t - LAG, (t - LAG) // 2, t % 2)
                with dve.Fori(2, STEPS // 2) as i:
                    for k in range(2):
                        agg(2 * i + k, i, k)
                        add(2 * i + k - 1, i - 1 + k, 1 - k)
                        dense(2 * i + k - LAG, i - 1, k)
                add(STEPS - 1, STEPS // 2 - 1, 1)
                last(dense)


def kernel(x, src, dst, edge_type_16, edge_type_8, L0_gnn_message_W, L0_gnn_message_b, L0_gnn_gru_w_ih,
           L0_gnn_gru_w_hh, L0_gnn_gru_b_ih, L0_gnn_gru_b_hh, L1_gnn_W, L1_gnn_b, L2_gnn_relation_weights,
           L2_gnn_self_weight, L2_gnn_bias, L3_gnn_id, L3_gnn_W1, L3_gnn_b1, L3_gnn_a1, L3_gnn_W2, L3_gnn_b2,
           L3_gnn_a2):
    import numpy as _np
    import concourse.bacc as _bacc
    from concourse import mybir as _mybir
    from concourse.bass_utils import run_bass_kernel_spmd as _run

    def edges(a, fill):
        a = _np.asarray(a)
        a = _np.concatenate([a, _np.full(STEPS * CH * P - EDGES, fill, a.dtype)])
        return _np.ascontiguousarray(a.reshape(STEPS * CH, P).T)

    def rows_first(a):
        a = _np.asarray(a)
        return _np.ascontiguousarray(a.transpose(1, 0, 2).reshape(a.shape[1], -1))

    def turned(a):
        return _np.ascontiguousarray(_np.asarray(a).T)

    x = _np.asarray(x)
    given = [
        ("x", _np.concatenate([x, _np.zeros((NP - NODES, F), x.dtype)])),
        ("src", edges(src, NODES)), ("dst", edges(dst, NODES)),
        ("type8", edges(edge_type_8, 0)), ("type16", edges(edge_type_16, 0)),
        ("w_msg", rows_first(L0_gnn_message_W)), ("b_msg", _np.asarray(L0_gnn_message_b).reshape(-1)),
        ("w_ih", turned(L0_gnn_gru_w_ih)), ("w_hh", turned(L0_gnn_gru_w_hh)),
        ("b_ih", _np.asarray(L0_gnn_gru_b_ih)), ("b_hh", _np.asarray(L0_gnn_gru_b_hh)),
        ("w_l1", turned(L1_gnn_W)), ("b_l1", _np.asarray(L1_gnn_b)),
        ("w_rel", rows_first(L2_gnn_relation_weights)), ("w_self", _np.asarray(L2_gnn_self_weight)),
        ("b_l2", _np.asarray(L2_gnn_bias)), ("id_vec", _np.asarray(L3_gnn_id)),
        ("w1", _np.asarray(L3_gnn_W1)), ("b1", _np.asarray(L3_gnn_b1)), ("a1", _np.asarray(L3_gnn_a1)),
        ("w2", _np.asarray(L3_gnn_W2)), ("b2", _np.asarray(L3_gnn_b2)), ("a2", _np.asarray(L3_gnn_a2)),
    ]
    nc = _bacc.Bacc("TRN2", target_bir_lowering=False, num_devices=1)
    args = [nc.dram_tensor(f"in_{n}", a.shape, _mybir.dt.from_np(a.dtype), kind="ExternalInput").ap() for n, a in given]
    out = nc.dram_tensor("out_x", (NP, F), _mybir.dt.float32, kind="ExternalOutput").ap()
    gnn_layers(nc, *args, out)
    r = _run(nc, [{f"in_{n}": _np.ascontiguousarray(a) for n, a in given}], core_ids=[0])
    return r.results[0]["out_x"][:NODES]
```

```python
import concourse.bass as bass
from concourse import mybir
from contextlib import ExitStack

P = 128
F = 128
NODES = 12500
EDGES = 212500
TILES = -(-NODES // P)
NP = TILES * P
CH = 17
STEPS = -(-EDGES // (CH * P))
CH_LAST = -(-EDGES // P) - (STEPS - 1) * CH
W = 144
WINDOWS = -(-NP // W)
ACC = max(NP + W, WINDOWS * W)
T8, T16 = 8, 16
ROW3 = 132
HID = 256
LAG = 2
EPS = 1e-5
assert STEPS == TILES and TILES % 2 == 0


def gnn_layers(nc, x_in, src, dst, type8, type16, w_msg, b_msg, w_ih, w_hh, b_ih, b_hh, w_l1, b_l1,
               w_rel, w_self, b_l2, id_vec, w1, b1, a1, w2, b2, a2, out):
    f32, i32 = mybir.dt.float32, mybir.dt.int32
    ALU, ACT = mybir.AluOpType, mybir.ActivationFunctionType
    ds = bass.ds

    def scratch(name, shape):
        return nc.dram_tensor(name, shape, f32, kind="Internal").ap()

    tab0 = scratch("table_typed8", (NP * T8, F))
    tab2 = scratch("table_typed16", (NP * T16, F))
    tab3 = scratch("table_scaled", (NP, ROW3))
    tab4 = scratch("table_conv2", (NP, F))
    h0_d, h1_d, h2_d = (scratch(f"h{n}_rows", (NP, F)) for n in range(3))
    x1_d, x2_d, x3_d = (scratch(f"x{n}_rows", (NP, F)) for n in (1, 2, 3))
    deg_d = scratch("degree", (TILES, P))

    ctx = ExitStack()
    with ctx:
        def sb(name, shape, dt=f32):
            return ctx.enter_context(nc.sbuf_tensor(name, shape, dt))

        def pb(name, shape):
            return ctx.enter_context(nc.psum_tensor(name, shape, f32))

        ORDER = ["W", "D", "T", 0, 1, 2, 3, 4]
        ONCE = ("W", "D")
        GIVEN = {
            "h_ready": ("T", 0, 1, 2, 3), "h_transposed": ("T", 0, 1, 2, 3), "hT_ready": ("T", 0, 1, 2),
            "products": ("T", 0, 1, 2, 3, 4), "rows_ready": ("T", 1),
            "stats": ("T", 0, 1, 2), "mean_var": ("T", 0, 1, 2), "rstd": ("T", 0, 1, 2), "std": ("T", 0, 1, 2),
            "norm_ready": ("T", 0, 1, 2), "rstd_scaled": (2,),
            "slot_ready": (0, 1, 2, 3, 4), "hot_ready": (0, 1, 2, 3, 4), "sums_ready": (0, 1, 2, 3, 4),
            "sums_added": (0, 1, 2, 3, 4), "gather_go": (0, 1, 2, 3, 4), "window_ready": (0, 3),
            "aux_added": (0, 3), "acc_zeroed": (0, 1, 2, 3, 4), "aT_ready": (0, 1, 2, 3, 4),
            "x_ready": (0, 1, 2, 4), "dinv_set": (2,),
            "rz_ready": (0,), "cand_in": (0,), "cand_ready": (0,), "r_hn": (0,), "h_less_n": (0,),
            "z_part": (0,), "gru_out": (0,),
            "mean": (1,), "mean_h": (1,), "h2_transposed": (1,), "h2T_ready": (1,), "rows_half": (1,),
            "rows_all": (1,), "rows_ready_act": (1,),
            "hid_ready": (3, 4), "conv_out": (3, 4), "below": (3, 4), "own_loop": (4,),
            "hid_transposed": (3,), "pT_ready": (3,), "products2": (3,),
            "g_slot_ready": (0, 1, 2, 3, 4),
        }
        SWEPT = {
            "g_numbered": (0, 1, 2, 3, 4), "g_hot_ready": (0, 1, 2, 3, 4), "g_sums_ready": (0, 1, 2, 3, 4),
            "g_added": (0, 1, 2, 3, 4),
        }
        SLOTS = {
            "x_loaded": {"T": 1}, "in_loaded": {0: 2, 1: 2, 2: 2, 3: 1, 4: 2},
            "h_stored": {"T": 1, 0: 1, 1: 1, 2: 1, 3: 1}, "x_stored": {0: 1, 1: 1, 2: 1, 4: 1},
            "rows_stored": {"T": 1, 1: 1},
        }
        made = {}

        def total(phase, name):
            if name == "done":
                return 1
            if name in GIVEN:
                return TILES if phase in GIVEN[name] else 0
            if name in SWEPT:
                return STEPS * WINDOWS if phase in SWEPT[name] else 0
            return 16 * SLOTS[name[:-1]].get(phase, 0) * (TILES // 2)

        def S(phase, name):
            own = phase in ONCE or name[:-1] == "rows_in"
            key = (phase, name) if own else name
            if key not in made:
                made[key] = ctx.enter_context(nc.semaphore(f"{phase}_{name}" if own else name))
            return made[key]

        def at(phase, name, value):
            if phase in ONCE or name[:-1] == "rows_in" or (isinstance(value, int) and value < 1):
                return S(phase, name), value
            return S(phase, name), sum(total(q, name) for q in ORDER[2:ORDER.index(phase)]) + value

        def after(eng, sem, value):
            if isinstance(value, int) and value < 1:
                return
            eng.wait_ge(sem, value)

        def hold(eng, name):
            eng.sem_inc(S("W", f"{name}_held"), 1)

        acc = sb("acc", [P, ACC])
        aux = sb("aux", [1, ACC])
        src_sb = sb("src_sb", [P, STEPS * CH], i32)
        dst_sb = sb("dst_sb", [P, STEPS * CH], i32)
        typed = sb("typed", [P, STEPS * CH], i32)
        rel = dst_sb[:, :].bitcast(f32)
        base_i = sb("base_i", [1, STEPS], i32)
        slot = [sb(f"slot{k}", [P, CH], i32) for k in range(2)]
        rows = [sb(f"rows{k}", [P, CH, ROW3]) for k in range(2)]
        hot = [sb(f"hot{k}", [P, CH, W]) for k in range(2)]
        node_i = sb("node_i", [P, W], i32)
        node = sb("node", [P, W])
        ident = sb("ident", [P, P])
        ones = sb("ones", [P, P])
        zero = sb("zero", [P, P])
        base_all = sb("base_all", [P, STEPS])
        node_w = sb("node_w", [P, W])
        bad_sb = sb("bad_sb", [P, 3])
        extreme = sb("extreme", [P, 4])
        ahead = sb("ahead", [1, STEPS])
        disorder_sb = sb("disorder_sb", [1, 1], i32)
        base_f = sb("base_f", [1, STEPS])
        wih_sb = sb("wih_sb", [P, 3 * F])
        whh_sb = sb("whh_sb", [P, 3 * F])
        bg_sb = sb("bg_sb", [1, 4 * F])
        bh_sb = sb("bh_sb", [1, 2 * F])
        wl1_sb = sb("wl1_sb", [P, F])
        bl1_sb = sb("bl1_sb", [1, F])
        wrel_sb = sb("wrel_sb", [P, T16 * F])
        wself_sb = sb("wself_sb", [P, F])
        bl2_sb = sb("bl2_sb", [1, F])
        id_sb = sb("id_sb", [8, 1])
        w1b_sb = sb("w1b_sb", [8, HID])
        idw_sb = sb("idw_sb", [1, HID])
        deg_t = sb("deg_t", [TILES, P])
        rdeg = sb("rdeg", [P, TILES])
        dinv = sb("dinv", [P, TILES])
        degm = sb("degm", [P, TILES])
        root = sb("root", [P, TILES])
        x_t = [sb(f"x_t{k}", [P, F]) for k in range(2)]
        h_t = [sb(f"h_t{k}", [P, ROW3]) for k in range(2)]
        xo_t = [sb(f"xo_t{k}", [P, F]) for k in range(2)]
        ho_t = [sb(f"ho_t{k}", [P, ROW3]) for k in range(2)]
        big_t = [sb(f"big_t{k}", [P, T16 * F]) for k in range(2)]
        wmsg_sb, bmsg_sb = big_t[0][:, T8 * F:2 * T8 * F], big_t[1][:, T8 * F:2 * T8 * F]
        w1a_sb, b1_sb, a1_sb = (big_t[1][:, n * HID:(n + 1) * HID] for n in range(3))
        w2_sb = big_t[1][:, 3 * HID:4 * HID].rearrange("p (k f) -> p k f", k=2)
        b2_sb, a2_sb = (big_t[1][:, 4 * HID + n * F:4 * HID + (n + 1) * F] for n in range(2))
        hid_a, hid_b, hid_c, pT = (big_t[0][:, n * HID:(n + 1) * HID] for n in range(4))
        hT = [sb(f"hT{k}", [P, P]) for k in range(2)]
        h2T = sb("h2T", [P, P])
        aT = sb("aT", [P, P])
        aux_t = sb("aux_t", [1, P])
        rz = sb("rz", [P, 2 * F])
        gate_a, gate_b, cand = (sb(n, [P, F]) for n in ("gate_a", "gate_b", "cand"))
        stats = [sb(f"stats{k}", [P, 6]) for k in range(2)]
        mv = [sb(f"mv{k}", [P, 2]) for k in range(2)]
        std = [sb(f"std{k}", [P, 1]) for k in range(2)]
        eps = sb("eps", [P, 1])
        rstd = [sb(f"rstd{k}", [P, 1]) for k in range(2)]
        nmr = [sb(f"nmr{k}", [P, 1]) for k in range(2)]

        big = pb("big", [P, 4 * 512])
        win = [pb(f"win{k}", [P, 512]) for k in range(2)]
        auxp = pb("auxp", [P, 512])
        trp = pb("trp", [P, 512])

        TABLE = [tab0, h1_d, tab2, tab3, tab4]
        INDEX = [typed, src_sb, typed, src_sb, src_sb]
        WIDTH = [F, F, F, ROW3, F]
        X_IN = [x_in, x1_d, x2_d, None, x3_d]
        H_IN = [h0_d, h1_d, h2_d, tab3, tab4]
        X_OUT = [x1_d, x2_d, x3_d, None, out]
        H_OUT = [h1_d, h2_d, tab3, tab4, None]
        AX = mybir.AxisListType
        AUX = (0, 3)

        def turns(eng, *stages, closing=None):
            def peeled(first, end):
                for s in range(first, end):
                    for lag, stage in closing if closing and s >= STEPS - 1 else stages:
                        if 0 <= s - lag < TILES:
                            stage(s - lag, (s - lag) // 2, (s - lag) % 2)

            peeled(-2, 4)
            with eng.Fori(2, TILES // 2 - 1) as i:
                for k in range(2):
                    for lag, stage in stages:
                        stage(2 * i + (k - lag), i + (k - lag) // 2, (k - lag) % 2)
            peeled(TILES - 2, TILES + 3)

        def all_tiles(eng, stage):
            for t in range(2):
                stage(t, 0, t)
            with eng.Fori(1, TILES // 2) as i:
                for k in range(2):
                    stage(2 * i + k, i, k)

        def chunks(t):
            return CH_LAST if isinstance(t, int) and t == STEPS - 1 else CH

        def by_order(eng, layers):
            eng.wait_ge(*at("W", "disorder", 1))
            disorder = eng.value_load(disorder_sb[0:1, 0:1], min_val=0, max_val=1)
            with eng.If(disorder == 0):
                layers(False)
            with eng.Else():
                layers(True)

        def tile_rows(ap, t):
            return ap[ds(t * P, P), :]

        def typed_rows(ap, t, n):
            return ap[ds(t * (P * n), P * n), :].rearrange("(p r) f -> p (r f)", r=n)

        block = ctx.enter_context(nc.Block())

        @block.sync
        def _(sp):
            def load_first(t, i, k):
                after(sp, *at("T", "h_ready", t - 1))
                if not isinstance(t, int):
                    hold(sp, "sp")
                sp.dma_start(x_t[k][:, :], tile_rows(x_in, t)).then_inc(S("T", f"x_loaded{k}"), 16)

            def store_h(t, i, k):
                sp.wait_ge(*at("T", "h_ready", t + 1))
                hold(sp, "sp")
                sp.dma_start(tile_rows(h0_d, t), ho_t[k][:, 0:F]).then_inc(S("T", f"h_stored{k}"), 16)

            def store_rows(t, i, k):
                sp.wait_ge(*at("T", "rows_ready", t + 1))
                hold(sp, "sp")
                sp.dma_start(typed_rows(tab0, t, T8), big_t[k][:, 0:T8 * F]).then_inc(S("T", f"rows_stored{k}"), 16)

            sp.dma_start(dst_sb[:, :], dst).then_inc(S("W", "edges"), 16)
            sp.dma_start(src_sb[:, :], src).then_inc(S("W", "edges"), 16)
            sp.dma_start(typed[:, :], type8).then_inc(S("W", "edges"), 16)
            turns(sp, (3, store_rows), (-2, load_first), (0, store_h))
            for k in range(2):
                sp.wait_ge(*at("T", f"h_stored{k}", 16 * (TILES // 2)))
                sp.wait_ge(*at("T", f"rows_stored{k}", 16 * (TILES // 2)))
            sp.sem_inc(S("T", "done"), 1)

            def load(p, t, i, k):
                after(sp, *at(p, "x_ready" if p != 3 else "h_transposed", t - 1))
                hold(sp, "sp")
                if X_IN[p] is not None:
                    sp.dma_start(x_t[k][:, :], tile_rows(X_IN[p], t)).then_inc(S(p, f"in_loaded{k}"), 16)
                hw = H_IN[p].shape[1]
                sp.dma_start(h_t[k][:, 0:hw], tile_rows(H_IN[p], t)).then_inc(S(p, f"in_loaded{k}"), 16)

            def store(p, t, i, k):
                if X_OUT[p] is not None:
                    sp.wait_ge(*at(p, "x_ready", t + 1))
                    hold(sp, "sp")
                    sp.dma_start(tile_rows(X_OUT[p], t), xo_t[k][:, :]).then_inc(S(p, f"x_stored{k}"), 16)
                if H_OUT[p] is not None:
                    hw = H_OUT[p].shape[1]
                    sp.wait_ge(*at(p, "h_ready", t + 1))
                    hold(sp, "sp")
                    if p == 2:
                        sp.wait_ge(*at(p, "dinv_set", t + 1))
                        hold(sp, "sp")
                    sp.dma_start(tile_rows(H_OUT[p], t), ho_t[k][:, 0:hw]).then_inc(S(p, f"h_stored{k}"), 16)
                if p == 1:
                    sp.wait_ge(*at(p, "rows_ready", t + 1))
                    hold(sp, "sp")
                    sp.wait_ge(*at(p, "rows_ready_act", t + 1))
                    hold(sp, "sp")
                    sp.dma_start(typed_rows(tab2, t, T16), big_t[k][:, :]).then_inc(S(p, f"rows_stored{k}"), 16)

            def layers(general):
                for p in range(5):
                    if p == 1:
                        sp.dma_start(typed[:, :], type16).then_inc(S("W", "type16"), 16)
                        sp.dma_start(deg_d.rearrange("(o t) p -> o (t p)", o=1), aux[0:1, 0:NP]).then_inc(S("D", "deg_out"), 16)
                        sp.wait_ge(*at("D", "deg_out", 16))
                        sp.dma_start(deg_t[:, :], deg_d).then_inc(S("D", "deg_in"), 16)

                    def load_p(t, i, k, p=p):
                        load(p, t, i, k)

                    def store_p(t, i, k, p=p):
                        store(p, t, i, k)

                    def load_store_p(t, i, k, p=p):
                        load(p, t, i, k)
                        store(p, t, i, k)

                    if general:
                        all_tiles(sp, load_store_p)
                    else:
                        turns(sp, (1, load_p), (LAG, store_p))
                    for k in range(2):
                        for name, used in (("x", X_OUT[p] is not None), ("h", H_OUT[p] is not None), ("rows", p == 1)):
                            if used:
                                sp.wait_ge(*at(p, f"{name}_stored{k}", 16 * (TILES // 2)))
                    sp.sem_inc(S(p, "done"), 1)

            by_order(sp, layers)

        @block.gpsimd
        def _(pool):
            pool.iota(node_i[:, :], [[1, W]], base=0, channel_multiplier=0).then_inc(S("W", "node_i"), 1)
            pool.memset(zero[:, :], 0.0)
            pool.memset(ones[:, :], 1.0).then_inc(S("W", "ones"), 1)
            pool.memset(eps[:, :], EPS).then_inc(S("W", "eps"), 1)
            pool.memset(ident[:, :], 0.0).then_inc(S("W", "zeroed"), 1)
            pool.wait_ge(*at("W", "zeroed", 1))
            pool.affine_select(out=ident[:, :], in_=ident[:, :], compare_op=ALU.not_equal, fill=1.0, base=0,
                               pattern=[[-1, P]], channel_multiplier=1).then_inc(S("W", "ident"), 1)
            pool.memset(aux[:, :], 0.0)
            pool.memset(acc[:, :], 0.0).then_inc(S("W", "acc_zero"), 1)

            def gather(p, k, n, signal):
                for c in range(n):
                    pool.indirect_dma_start(
                        rows[k][:, c, 0:WIDTH[p]], None, TABLE[p],
                        bass.IndirectOffsetOnAxis(ap=slot[k][:, c:c + 1], axis=0),
                    ).then_inc(S(p, signal), 16)

            def layers(general):
                for p in range(5):
                    pool.wait_ge(*at("T" if p == 0 else p - 1, "done", 1))

                    def agg(t, i, k, p=p):
                        pool.wait_ge(*at(p, "slot_ready", t + 1))
                        after(pool, *at(p, "sums_ready", t - 1))
                        hold(pool, "pool")
                        gather(p, k, chunks(t), f"rows_in{k}")

                    def sweep(s, p=p):
                        pool.wait_ge(*at(p, "g_slot_ready", s + 1))
                        after(pool, *at(p, "g_added", WINDOWS * s))
                        hold(pool, "pool")
                        gather(p, 0, CH, "rows_in2")

                    if general:
                        sweep(0)
                        with pool.Fori(1, STEPS) as s:
                            sweep(s)
                    else:
                        turns(pool, (0, agg))

            by_order(pool, layers)

        @block.scalar
        def _(act):
            def load(dst_ap, src_ap, group):
                act.dma_start(dst_ap, src_ap).then_inc(S("W", group), 16)

            def spread(vec):
                return vec.rearrange("(o n) -> o n", o=1)

            load(wmsg_sb, w_msg, "msg")
            load(bmsg_sb, b_msg.partition_broadcast(P), "msg")
            load(bg_sb[:, 0:3 * F], spread(b_ih), "gru")
            load(bg_sb[:, 3 * F:4 * F], spread(b_hh)[:, 2 * F:3 * F], "gru")
            load(bh_sb[:, :], spread(b_hh)[:, 0:2 * F], "gru")
            load(wih_sb[:, :], w_ih, "gru")
            load(whh_sb[:, :], w_hh, "gru")
            load(wl1_sb[:, :], w_l1, "rest")
            load(bl1_sb[:, :], spread(b_l1), "rest")
            load(wrel_sb[:, :], w_rel, "rest")
            load(wself_sb[:, :], w_self, "rest")
            load(bl2_sb[:, :], spread(b_l2), "rest")
            load(id_sb[:, :], id_vec.rearrange("(n o) -> n o", o=1), "rest")
            load(w1b_sb[:, :], w1[F:F + 8, :], "rest")

            def deviation(ph, t, k):
                act.wait_ge(*at(ph, "mean_var", t + 1))
                act.activation(std[k][:, :], mv[k][:, 1:2], ACT.Sqrt, bias=eps[:, 0:1]).then_inc(S(ph, "std"), 1)

            def normalise(ph, t, k, x_ap, h_ap):
                act.wait_ge(*at(ph, "norm_ready", t + 1))
                act.activation(h_ap, x_ap, ACT.Relu, bias=nmr[k][:, 0:1], scale=rstd[k][:, 0:1]).then_inc(S(ph, "h_ready"), 1)

            def norm_first(t, i, k):
                deviation("T", t, k)
                after(act, *at("T", f"h_stored{k}", 16 * i))
                after(act, *at("T", "h_transposed", t - 1))
                normalise("T", t, k, x_t[k][:, :], ho_t[k][:, 0:F])

            def copy_first(t, i, k):
                act.wait_ge(*at("T", "h_transposed", t + 1))
                after(act, *at("T", "products", t - 1))
                act.copy(hT[k][:, :], trp[:, 0:P]).then_inc(S("T", "hT_ready"), 1)

            act.wait_ge(*at("W", "eps", 1))
            turns(act, (0, norm_first), (1, copy_first))

            def layers(general):
                for p in range(5):
                    def agg(t, i, k, p=p):
                        after(act, *at(p, f"rows_in{k}", 16 * CH * i))
                        act.copy(slot[k][:, :], INDEX[p][:, ds(t * CH, CH)]).then_inc(S(p, "slot_ready"), 1)

                    def dense(t, i, k, p=p):
                        if p in (0, 1, 2):
                            act.wait_ge(*at(p, "h_transposed", t + 1))
                            act.copy(hT[0][:, :], trp[:, 0:P]).then_inc(S(p, "hT_ready"), 1)
                        if p == 0:
                            act.wait_ge(*at(p, "products", t + 1))
                            act.activation(rz[:, :], big[:, 0:2 * F], ACT.Sigmoid).then_inc(S(p, "rz_ready"), 1)
                            act.wait_ge(*at(p, "cand_in", t + 1))
                            act.activation(cand[:, :], gate_b[:, :], ACT.Tanh).then_inc(S(p, "cand_ready"), 1)
                        if p in (0, 1, 2):
                            after(act, *at(p, f"h_stored{k}", 16 * i))
                            deviation(p, t, k)
                            normalise(p, t, k, xo_t[k][:, :], ho_t[k][:, 0:F])
                        if p == 1:
                            act.wait_ge(*at(p, "h2_transposed", t + 1))
                            act.copy(h2T[:, :], trp[:, 0:P]).then_inc(S(p, "h2T_ready"), 1)
                            after(act, *at(p, f"rows_stored{k}", 16 * i))
                            act.wait_ge(*at(p, "rows_half", t + 1))
                            act.copy(big_t[k][:, 0:8 * F], big[:, 0:8 * F]).then_inc(S(p, "rows_ready_act"), 1)
                        if p == 3:
                            act.wait_ge(*at(p, "hid_transposed", t + 1))
                            act.copy(pT, trp[:, 0:HID]).then_inc(S(p, "pT_ready"), 1)
                            act.wait_ge(*at(p, "products2", t + 1))
                            after(act, *at(p, f"h_stored{k}", 16 * i))
                            act.activation(ho_t[k][:, 0:F], big[:, 512:512 + F], ACT.Identity,
                                           scale=dinv[:, ds(t, 1)]).then_inc(S(p, "h_ready"), 1)

                    act.wait_ge(*at("T" if p == 0 else p - 1, "done", 1))
                    if p == 0:
                        act.wait_ge(*at("W", "idx8", 1))
                    if p == 1:
                        act.wait_ge(*at("D", "degm", 1))
                        act.activation(root[:, :], trp[:, 0:TILES], ACT.Sqrt, bias=ones[:, 0:1]).then_inc(S("D", "root"), 1)
                    if p == 2:
                        act.wait_ge(*at("W", "idx16", 1))
                        load(w1a_sb, w1[0:F, :], "late")
                        load(b1_sb, b1.partition_broadcast(P), "late")
                        load(a1_sb, a1.partition_broadcast(P), "late")
                        load(w2_sb, w2.rearrange("(k p) f -> p k f", k=2), "late")
                        load(b2_sb, b2.partition_broadcast(P), "late")
                        load(a2_sb, a2.partition_broadcast(P), "late")
                    def sweep(s, p=p):
                        after(act, *at(p, "rows_in2", 16 * CH * s))
                        act.copy(slot[0][:, :], INDEX[p][:, ds(s * CH, CH)]).then_inc(S(p, "g_slot_ready"), 1)

                    if general:
                        sweep(0)
                        with act.Fori(1, STEPS) as s:
                            sweep(s)
                        all_tiles(act, dense)
                    else:
                        turns(act, (-1, agg), (LAG, dense))

            by_order(act, layers)

        @block.tensor
        def _(pe):
            mm = nc.tensor.matmul
            pe.wait_ge(*at("W", "ones", 1))
            pe.wait_ge(*at("W", "ident", 1))
            pe.wait_ge(*at("W", "base_f", 1))
            mm(auxp[:, 0:STEPS], ones[0:1, :], base_f[:, :], start=True, stop=True).then_inc(S("W", "base_all"), 1)
            pe.wait_ge(*at("W", "bad", 3))
            mm(trp[0:1, 0:3], ones[:, 0:1], bad_sb[:, :], start=True, stop=True).then_inc(S("W", "bad_sum"), 1)
            pe.wait_ge(*at("W", "disorder", 1))
            pe.wait_ge(*at("W", "msg", 32))

            def transpose_first(t, i, k):
                pe.wait_ge(*at("T", "h_ready", t + 1))
                after(pe, *at("T", "hT_ready", t))
                nc.tensor.transpose(trp[:, 0:P], ho_t[k][:, 0:F], ident[:, :]).then_inc(S("T", "h_transposed"), 1)

            def products_first(t, i, k):
                pe.wait_ge(*at("T", "hT_ready", t + 1))
                after(pe, *at("T", "rows_ready", t - 1))
                for j in range(2):
                    last_mm = mm(big[:, (2 * k + j) * 512:(2 * k + j + 1) * 512], hT[k][:, :],
                                 wmsg_sb[:, j * 512:(j + 1) * 512], start=True, stop=True)
                last_mm.then_inc(S("T", "products"), 1)

            turns(pe, (1, transpose_first), (2, products_first))

            pe.wait_ge(*at("W", "gru", 16 * 5))
            pe.wait_ge(*at("W", "bg", 1))
            pe.wait_ge(*at("W", "rest", 16 * 7))
            pe.wait_ge(*at("W", "rel", 1))
            mm(auxp[0:1, 0:HID], id_sb[:, :], w1b_sb[:, :], start=True, stop=True).then_inc(S("W", "idw_mm"), 1)
            pe.wait_ge(*at("W", "idw", 1))

            def layers(general):
                for p in range(5):
                    pe.wait_ge(*at("T" if p == 0 else p - 1, "done", 1))
                    if p == 3:
                        pe.wait_ge(*at("W", "late", 16 * 6))
                    if p == 1:
                        pe.wait_ge(*at("D", "deg_in", 16))
                        nc.tensor.transpose(trp[:, 0:TILES], deg_t[:, :], ident[0:TILES, 0:TILES]).then_inc(S("D", "deg_cols"), 1)
                        pe.wait_ge(*at("D", "deg_done", 1))

                    def add_up(target, values, hots, n, first, end):
                        for c in range(first, end):
                            last_mm = mm(target, values(c), hots[:, c, :], start=c == 0, stop=c == n - 1)
                        return last_mm

                    def row(k, p=p):
                        return lambda c: rows[k][:, c, 0:F]

                    def weight(k, p=p):
                        return lambda c: ones[:, 0:1] if p == 0 else rows[k][:, c, F:F + 1]

                    def sums_begin(t, i, k, p=p):
                        pe.wait_ge(*at(p, f"rows_in{k}", 16 * CH * i + 16 * chunks(t)))
                        pe.wait_ge(*at(p, "hot_ready", t + 1))
                        after(pe, *at(p, "sums_added", t - 1))
                        add_up(win[k][:, 0:W], row(k), hot[k], chunks(t), 0, CH // 2)

                    def sums_end(t, i, k, p=p):
                        add_up(win[k][:, 0:W], row(k), hot[k], chunks(t), CH // 2, chunks(t))\
                            .then_inc(S(p, "window_ready" if p in AUX else "sums_ready"), 1)

                    def aux_begin(t, i, k, p=p):
                        after(pe, *at(p, "aux_added", t))
                        add_up(auxp[0:1, 0:W], weight(k), hot[k], chunks(t), 0, CH // 2)

                    def aux_end(t, i, k, p=p):
                        add_up(auxp[0:1, 0:W], weight(k), hot[k], chunks(t), CH // 2, chunks(t))\
                            .then_inc(S(p, "sums_ready"), 1)

                    def sweep(s, p=p):
                        pe.wait_ge(*at(p, "rows_in2", 16 * CH * (s + 1)))
                        hold(pe, "pe")
                        with pe.Fori(0, WINDOWS) as w:
                            pe.wait_ge(*at(p, "g_hot_ready", s * WINDOWS + w + 1))
                            if p in AUX:
                                add_up(auxp[0:1, 0:W], weight(0), hot[0], CH, 0, CH)
                            add_up(win[0][:, 0:W], row(0), hot[0], CH, 0, CH).then_inc(S(p, "g_sums_ready"), 1)

                    def transpose_in(t, i, k, p=p):
                        if p != 4:
                            n_in = 1 if X_IN[p] is None else 2
                            pe.wait_ge(*at(p, f"in_loaded{k}", 16 * n_in * (i + 1)))
                            last_mm = nc.tensor.transpose(trp[:, 0:P], h_t[k][:, 0:F], ident[:, :])
                            if p == 3:
                                last_mm = nc.tensor.transpose(trp[0:1, P:2 * P], h_t[k][:, F:F + 1], ident[:, :])
                            last_mm.then_inc(S(p, "h_transposed"), 1)

                    def products(t, i, k, p=p):
                        pe.wait_ge(*at(p, "aT_ready", t + 1))
                        if p == 0:
                            mm(big[:, 0:4 * F], ones[0:1, :], bg_sb[:, :], start=True, stop=False)
                            mm(big[:, 0:3 * F], aT[:, :], wih_sb[:, :], start=False, stop=False)
                            pe.wait_ge(*at(p, "hT_ready", t + 1))
                            mm(big[:, 0:2 * F], hT[0][:, :], whh_sb[:, 0:2 * F], start=False, stop=False)
                            mm(big[:, 3 * F:4 * F], hT[0][:, :], whh_sb[:, 2 * F:3 * F], start=False, stop=True)\
                                .then_inc(S(p, "products"), 1)
                        if p == 1:
                            after(pe, *at(p, "rows_ready_act", t))
                            mm(big[:, 0:F], aT[:, :], wl1_sb[:, :], start=True, stop=True)
                            mm(big[:, 512:512 + F], ones[0:1, :], bl1_sb[:, :], start=True, stop=False)
                            pe.wait_ge(*at(p, "hT_ready", t + 1))
                            mm(big[:, 512:512 + F], hT[0][:, :], wl1_sb[:, :], start=False, stop=True)\
                                .then_inc(S(p, "products"), 1)
                        if p == 2:
                            mm(big[:, 0:F], ones[0:1, :], bl2_sb[:, :], start=True, stop=False)
                            mm(big[:, 0:F], aT[:, :], ident[:, :], start=False, stop=False)
                            pe.wait_ge(*at(p, "hT_ready", t + 1))
                            mm(big[:, 0:F], hT[0][:, :], wself_sb[:, :], start=False, stop=True).then_inc(S(p, "products"), 1)
                        if p == 3:
                            mm(big[:, 0:HID], aT[:, :], w1a_sb, start=True, stop=False)
                            mm(big[:, 0:HID], aux_t[:, :], idw_sb[:, :], start=False, stop=True).then_inc(S(p, "products"), 1)
                        if p == 4:
                            nc.tensor.transpose(big[:, 0:F], aT[:, :], ident[:, :]).then_inc(S(p, "products"), 1)

                    def transpose_out(t, i, k, p=p):
                        if p == 1:
                            pe.wait_ge(*at(p, "h_ready", t + 1))
                            nc.tensor.transpose(trp[:, 0:P], ho_t[k][:, 0:F], ident[:, :]).then_inc(S(p, "h2_transposed"), 1)
                        if p == 3:
                            pe.wait_ge(*at(p, "hid_ready", t + 1))
                            for j in range(2):
                                last_mm = nc.tensor.transpose(trp[:, j * P:(j + 1) * P], hid_c[:, j * P:(j + 1) * P], ident[:, :])
                            last_mm.then_inc(S(p, "hid_transposed"), 1)

                    def products_out(t, i, k, p=p):
                        if p == 1:
                            pe.wait_ge(*at(p, "h2T_ready", t + 1))
                            for j in range(4):
                                last_mm = mm(big[:, j * 512:(j + 1) * 512], h2T[:, :], wrel_sb[:, j * 512:(j + 1) * 512],
                                             start=True, stop=True)
                                if j == 1:
                                    last_mm.then_inc(S(p, "rows_half"), 1)
                            last_mm.then_inc(S(p, "rows_all"), 1)
                        if p == 3:
                            pe.wait_ge(*at(p, "pT_ready", t + 1))
                            for j in range(2):
                                last_mm = mm(big[:, 512:512 + F], pT[:, j * P:(j + 1) * P], w2_sb[:, j, :],
                                             start=j == 0, stop=j == 1)
                            last_mm.then_inc(S(p, "products2"), 1)

                    def dense(t, i, k):
                        for part in (transpose_in, products, transpose_out, products_out):
                            part(t, i, k)

                    sums = [(0, sums_begin), (0, sums_end)] + [(0, aux_begin), (0, aux_end)] * (p in AUX)

                    if general:
                        with pe.Fori(0, STEPS) as s:
                            sweep(s)
                        all_tiles(pe, dense)
                    else:
                        aux_parts = [(0, aux_begin)], [(0, aux_end)]
                        turns(pe, (LAG, transpose_in), (0, sums_begin), (LAG, products), (0, sums_end),
                              *(aux_parts[0] if p in AUX else []), (LAG, transpose_out),
                              *(aux_parts[1] if p in AUX else []), (LAG, products_out),
                              closing=[(LAG, dense)] + sums)

            by_order(pe, layers)

        @block.vector
        def _(dve):
            V = nc.vector
            dve.wait_ge(*at("W", "node_i", 1))
            V.tensor_copy(node[:, :], node_i[:, :]).then_inc(S("W", "node"), 1)

            def moments(ph, t, k, x_ap):
                V.bn_stats(stats[k][:, :], x_ap).then_inc(S(ph, "stats"), 1)
                dve.wait_ge(*at(ph, "stats", t + 1))
                hold(dve, "dve")
                V.bn_aggr(mv[k][:, :], stats[k][:, :]).then_inc(S(ph, "mean_var"), 1)

            def normalise(ph, t, k, scale=None):
                dve.wait_ge(*at(ph, "std", t + 1))
                V.reciprocal(rstd[k][:, :], std[k][:, :]).then_inc(S(ph, "rstd"), 1)
                dve.wait_ge(*at(ph, "rstd", t + 1))
                if scale is not None:
                    V.tensor_scalar(rstd[k][:, :], rstd[k][:, :], scale, None, ALU.mult).then_inc(S(ph, "rstd_scaled"), 1)
                    dve.wait_ge(*at(ph, "rstd_scaled", t + 1))
                V.scalar_tensor_tensor(out=nmr[k][:, :], in0=mv[k][:, 0:1], scalar=-1.0, in1=rstd[k][:, :],
                                       op0=ALU.mult, op1=ALU.mult).then_inc(S(ph, "norm_ready"), 1)

            def moments_first(t, i, k):
                dve.wait_ge(*at("T", f"x_loaded{k}", 16 * (i + 1)))
                after(dve, *at("T", "h_ready", t - 1))
                moments("T", t, k, x_t[k][:, :])

            def rows_first(t, i, k):
                dve.wait_ge(*at("T", "products", t + 1))
                after(dve, *at("T", f"rows_stored{k}", 16 * i))
                V.tensor_tensor(big_t[k][:, 0:T8 * F], big[:, k * 1024:(k + 1) * 1024], bmsg_sb, ALU.add)\
                    .then_inc(S("T", "rows_ready"), 1)

            dve.wait_ge(*at("W", "edges", 48))
            V.tensor_copy(base_i[:, :], dst_sb[0:1, :].rearrange("o (s c) -> o s c", c=CH)[:, :, 0])
            V.tensor_copy(base_f[:, :], dst_sb[0:1, :].rearrange("o (s c) -> o s c", c=CH)[:, :, 0]).then_inc(S("W", "base_f"), 1)
            V.scalar_tensor_tensor(out=typed[:, :], in0=src_sb[:, :], scalar=float(T8), in1=typed[:, :],
                                   op0=ALU.mult, op1=ALU.add).then_inc(S("W", "idx8"), 1)
            dve.wait_ge(*at("W", "base_all", 1))
            V.tensor_tensor(rel.rearrange("p (s c) -> p s c", c=CH), dst_sb[:, :].rearrange("p (s c) -> p s c", c=CH),
                            auxp[:, 0:STEPS].unsqueeze(2).to_broadcast([P, STEPS, CH]), ALU.subtract).then_inc(S("W", "rel"), 1)
            V.memset(bad_sb[:, :], 0.0).then_inc(S("W", "bad_zero"), 1)
            V.tensor_copy(base_all[:, :], auxp[:, 0:STEPS])
            dve.wait_ge(*at("W", "rel", 1))
            V.tensor_reduce(extreme[:, 0:1], rel[:, 0:(STEPS - 1) * CH + CH_LAST], AX.X, ALU.max)
            V.tensor_reduce(extreme[:, 1:2], rel[:, 0:(STEPS - 1) * CH + CH_LAST], AX.X, ALU.min).then_inc(S("W", "extreme"), 1)
            dve.wait_ge(*at("W", "node", 1))
            V.scalar_tensor_tensor(out=ahead[:, :], in0=node[0:1, 0:STEPS], scalar=-float(P), in1=base_f[:, :],
                                   op0=ALU.mult, op1=ALU.add).then_inc(S("W", "ahead"), 1)
            dve.wait_ge(*at("W", "ahead", 1))
            V.tensor_reduce(extreme[0:1, 2:3], ahead[:, :], AX.X, ALU.min).then_inc(S("W", "extreme"), 1)
            dve.wait_ge(*at("W", "extreme", 2))
            dve.wait_ge(*at("W", "bad_zero", 1))
            V.tensor_scalar(bad_sb[:, 0:1], extreme[:, 0:1], float(W), None, ALU.is_ge).then_inc(S("W", "bad"), 1)
            V.tensor_scalar(bad_sb[:, 1:2], extreme[:, 1:2], 0.0, None, ALU.is_lt).then_inc(S("W", "bad"), 1)
            V.tensor_scalar(bad_sb[0:1, 2:3], extreme[0:1, 2:3], -float(P), None, ALU.is_lt).then_inc(S("W", "bad"), 1)
            dve.wait_ge(*at("W", "bad_sum", 1))
            V.tensor_reduce(extreme[0:1, 3:4], trp[0:1, 0:3], AX.X, ALU.add).then_inc(S("W", "bad_total"), 1)
            dve.wait_ge(*at("W", "bad_total", 1))
            V.tensor_scalar(disorder_sb[:, :], extreme[0:1, 3:4], 1.0, None, ALU.min).then_inc(S("W", "disorder"), 1)
            dve.wait_ge(*at("W", "gru", 16 * 5))
            V.tensor_tensor(bg_sb[:, 0:2 * F], bg_sb[:, 0:2 * F], bh_sb[:, :], ALU.add).then_inc(S("W", "bg"), 1)
            dve.wait_ge(*at("W", "msg", 32))
            turns(dve, (0, moments_first), (3, rows_first), (0, lambda t, i, k: normalise("T", t, k)))
            dve.wait_ge(*at("W", "idw_mm", 1))
            V.tensor_copy(idw_sb[:, :], auxp[0:1, 0:HID]).then_inc(S("W", "idw"), 1)
            dve.wait_ge(*at("W", "node", 1))
            dve.wait_ge(*at("W", "acc_zero", 1))
            dve.wait_ge(*at("W", "rest", 16 * 7))

            def layers(general):
                for p in range(5):
                    dve.wait_ge(*at("T" if p == 0 else p - 1, "done", 1))
                    if p == 1:
                        dve.wait_ge(*at("W", "type16", 16))
                        V.scalar_tensor_tensor(out=typed[:, :], in0=src_sb[:, :], scalar=float(T16), in1=typed[:, :],
                                               op0=ALU.mult, op1=ALU.add).then_inc(S("W", "idx16"), 1)
                        dve.wait_ge(*at("D", "deg_cols", 1))
                        V.tensor_scalar(degm[:, :], trp[:, 0:TILES], 1.0, None, ALU.max).then_inc(S("D", "degm"), 1)
                        dve.wait_ge(*at("D", "root", 1))
                        V.reciprocal(dinv[:, :], root[:, :])
                        dve.wait_ge(*at("D", "degm", 1))
                        V.reciprocal(rdeg[:, :], degm[:, :]).then_inc(S("D", "deg_done"), 1)
                        dve.wait_ge(*at("D", "deg_done", 1))
                    if p == 3:
                        dve.wait_ge(*at("W", "late", 16 * 6))
                    if p == 2:
                        V.memset(aux[:, :], 0.0).then_inc(S("D", "aux_zero"), 1)
                        dve.wait_ge(*at("D", "aux_zero", 1))

                    def one_hot(k, column, n, numbers):
                        return V.tensor_tensor(
                            hot[k][:, 0:n, :], numbers[:, :].unsqueeze(1).to_broadcast([P, n, W]),
                            rel[:, ds(column, n)].unsqueeze(2).to_broadcast([P, n, W]), ALU.is_equal)

                    def add_window(target, columns, sums):
                        return V.tensor_tensor(target[:, columns], target[:, columns], sums, ALU.add)

                    def agg(t, i, k, p=p):
                        after(dve, *at(p, "sums_ready", t - 1))
                        one_hot(k, t * CH, chunks(t), node).then_inc(S(p, "hot_ready"), 1)

                    def add(t, i, k, p=p):
                        base = dve.value_load(base_i[0:1, ds(t, 1)], min_val=0, max_val=NP)
                        after(dve, *at(p, "sums_added", t))
                        dve.wait_ge(*at(p, "window_ready" if p in AUX else "sums_ready", t + 1))
                        add_window(acc, ds(base, W), win[k][:, 0:W]).then_inc(S(p, "sums_added"), 1)
                        if p in AUX:
                            after(dve, *at(p, "aux_added", t))
                            dve.wait_ge(*at(p, "sums_ready", t + 1))
                            add_window(aux, ds(base, W), auxp[0:1, 0:W]).then_inc(S(p, "aux_added"), 1)

                    def sweep(s, p=p):
                        def window(w, first):
                            n = s * WINDOWS + w
                            dve.wait_ge(*at(p, "g_numbered", n + 1))
                            one_hot(0, s * CH, CH, node_w).then_inc(S(p, "g_hot_ready"), 1)
                            dve.wait_ge(*at(p, "g_sums_ready", n + 1))
                            if p in AUX:
                                add_window(aux, ds(w * W, W), auxp[0:1, 0:W])
                            add_window(acc, ds(w * W, W), win[0][:, 0:W]).then_inc(S(p, "g_added"), 1)

                        V.tensor_scalar(node_w[:, :], node[:, :], base_all[:, ds(s, 1)], None, ALU.subtract)\
                            .then_inc(S(p, "g_numbered"), 1)
                        window(0, True)
                        with dve.Fori(1, WINDOWS) as w:
                            V.tensor_scalar(node_w[:, :], node_w[:, :], float(W), None, ALU.add)\
                                .then_inc(S(p, "g_numbered"), 1)
                            window(w, False)

                    def dense(t, i, k, p=p):
                        tile_acc = acc[:, ds(t * P, P)]
                        if not general:
                            done = min(t + LAG, STEPS) if isinstance(t, int) else t + LAG
                            dve.wait_ge(*at(p, "sums_added", done))
                            if p == 3:
                                dve.wait_ge(*at(p, "aux_added", done))
                        if p == 3:
                            dve.wait_ge(*at(p, "h_transposed", t + 1))
                            V.tensor_tensor(aT[:, :], tile_acc, trp[:, 0:P], ALU.add)
                            V.tensor_tensor(aux_t[:, :], aux[:, ds(t * P, P)], trp[0:1, P:2 * P], ALU.add)\
                                .then_inc(S(p, "aT_ready"), 1)
                        else:
                            V.tensor_scalar(aT[:, :], tile_acc, 1.0, None, ALU.mult).then_inc(S(p, "aT_ready"), 1)
                        dve.wait_ge(*at(p, "aT_ready", t + 1))
                        V.tensor_scalar(tile_acc, zero[:, :], 1.0, None, ALU.mult).then_inc(S(p, "acc_zeroed"), 1)
                        n_in = 1 if X_IN[p] is None else 2
                        dve.wait_ge(*at(p, f"in_loaded{k}", 16 * n_in * (i + 1)))
                        if X_OUT[p] is not None:
                            after(dve, *at(p, f"x_stored{k}", 16 * i))
                        if p == 0:
                            dve.wait_ge(*at(p, "rz_ready", t + 1))
                            V.tensor_tensor(gate_a[:, :], rz[:, 0:F], big[:, 3 * F:4 * F], ALU.mult).then_inc(S(p, "r_hn"), 1)
                            dve.wait_ge(*at(p, "r_hn", t + 1))
                            V.tensor_tensor(gate_b[:, :], gate_a[:, :], big[:, 2 * F:3 * F], ALU.add).then_inc(S(p, "cand_in"), 1)
                            dve.wait_ge(*at(p, "cand_ready", t + 1))
                            V.tensor_tensor(gate_a[:, :], h_t[k][:, 0:F], cand[:, :], ALU.subtract).then_inc(S(p, "h_less_n"), 1)
                            dve.wait_ge(*at(p, "h_less_n", t + 1))
                            V.tensor_tensor(gate_b[:, :], rz[:, F:2 * F], gate_a[:, :], ALU.mult).then_inc(S(p, "z_part"), 1)
                            dve.wait_ge(*at(p, "z_part", t + 1))
                            V.tensor_tensor(gate_a[:, :], gate_b[:, :], cand[:, :], ALU.add).then_inc(S(p, "gru_out"), 1)
                            dve.wait_ge(*at(p, "gru_out", t + 1))
                            V.tensor_tensor(xo_t[k][:, :], gate_a[:, :], x_t[k][:, :], ALU.add).then_inc(S(p, "x_ready"), 1)
                        if p == 1:
                            dve.wait_ge(*at(p, "products", t + 1))
                            V.tensor_scalar(gate_a[:, :], big[:, 0:F], rdeg[:, ds(t, 1)], None, ALU.mult).then_inc(S(p, "mean"), 1)
                            dve.wait_ge(*at(p, "mean", t + 1))
                            V.tensor_tensor(gate_b[:, :], gate_a[:, :], big[:, 512:512 + F], ALU.add).then_inc(S(p, "mean_h"), 1)
                            dve.wait_ge(*at(p, "mean_h", t + 1))
                            V.scalar_tensor_tensor(out=xo_t[k][:, :], in0=gate_b[:, :], scalar=0.0, in1=x_t[k][:, :],
                                                   op0=ALU.max, op1=ALU.add).then_inc(S(p, "x_ready"), 1)
                        if p == 2:
                            dve.wait_ge(*at(p, "products", t + 1))
                            V.scalar_tensor_tensor(out=xo_t[k][:, :], in0=big[:, 0:F], scalar=0.0, in1=x_t[k][:, :],
                                                   op0=ALU.max, op1=ALU.add).then_inc(S(p, "x_ready"), 1)
                        if p in (0, 1, 2):
                            dve.wait_ge(*at(p, "x_ready", t + 1))
                            if p == 2:
                                after(dve, *at(p, f"h_stored{k}", 16 * i))
                                V.tensor_scalar(ho_t[k][:, F:ROW3], ones[:, 0:ROW3 - F], dinv[:, ds(t, 1)], None, ALU.mult)\
                                    .then_inc(S(p, "dinv_set"), 1)
                            after(dve, *at(p, "h_ready", t - 1))
                            moments(p, t, k, xo_t[k][:, :])
                            normalise(p, t, k, dinv[:, ds(t, 1)] if p == 2 else None)
                        if p == 1:
                            dve.wait_ge(*at(p, "rows_all", t + 1))
                            after(dve, *at(p, f"rows_stored{k}", 16 * i))
                            V.tensor_copy(big_t[k][:, 8 * F:], big[:, 8 * F:]).then_inc(S(p, "rows_ready"), 1)
                        if p in (3, 4):
                            n, o, b_sb, a_sb = (HID, "dinv_b", b1_sb, a1_sb) if p == 3 else (F, "dinv_b", b2_sb, a2_sb)
                            dve.wait_ge(*at(p, "products", t + 1))
                            pre = big[:, 0:n]
                            if p == 4:
                                V.tensor_tensor(hid_b[:, 0:n], big[:, 0:n], h_t[k][:, 0:F], ALU.add).then_inc(S(p, "own_loop"), 1)
                                dve.wait_ge(*at(p, "own_loop", t + 1))
                                pre = hid_b[:, 0:n]
                            V.scalar_tensor_tensor(out=hid_a[:, 0:n], in0=pre, scalar=dinv[:, ds(t, 1)], in1=b_sb,
                                                   op0=ALU.mult, op1=ALU.add).then_inc(S(p, "conv_out"), 1)
                            dve.wait_ge(*at(p, "conv_out", t + 1))
                            V.scalar_tensor_tensor(out=hid_b[:, 0:n], in0=hid_a[:, 0:n], scalar=0.0, in1=a_sb,
                                                   op0=ALU.min, op1=ALU.mult).then_inc(S(p, "below"), 1)
                            dve.wait_ge(*at(p, "below", t + 1))
                            V.scalar_tensor_tensor(out=hid_c[:, 0:n], in0=hid_a[:, 0:n], scalar=0.0, in1=hid_b[:, 0:n],
                                                   op0=ALU.max, op1=ALU.add).then_inc(S(p, "hid_ready"), 1)
                        if p == 4:
                            dve.wait_ge(*at(p, "hid_ready", t + 1))
                            V.tensor_tensor(xo_t[k][:, :], hid_c[:, 0:F], x_t[k][:, :], ALU.add).then_inc(S(p, "x_ready"), 1)

                    if general:
                        with dve.Fori(0, STEPS) as s:
                            sweep(s)
                        dve.wait_ge(*at(p, "g_added", STEPS * WINDOWS))
                        all_tiles(dve, dense)
                    else:
                        turns(dve, (1, add), (-1, agg), (LAG, dense))

            by_order(dve, layers)


def kernel(x, src, dst, edge_type_16, edge_type_8, L0_gnn_message_W, L0_gnn_message_b, L0_gnn_gru_w_ih,
           L0_gnn_gru_w_hh, L0_gnn_gru_b_ih, L0_gnn_gru_b_hh, L1_gnn_W, L1_gnn_b, L2_gnn_relation_weights,
           L2_gnn_self_weight, L2_gnn_bias, L3_gnn_id, L3_gnn_W1, L3_gnn_b1, L3_gnn_a1, L3_gnn_W2, L3_gnn_b2,
           L3_gnn_a2):
    import numpy as _np
    import concourse.bacc as _bacc
    from concourse import mybir as _mybir
    from concourse.bass_utils import run_bass_kernel_spmd as _run

    def edges(a, fill):
        a = _np.asarray(a)
        a = _np.concatenate([a, _np.full(STEPS * CH * P - EDGES, fill, a.dtype)])
        return _np.ascontiguousarray(a.reshape(STEPS * CH, P).T)

    def rows_first(a):
        a = _np.asarray(a)
        return _np.ascontiguousarray(a.transpose(1, 0, 2).reshape(a.shape[1], -1))

    def turned(a):
        return _np.ascontiguousarray(_np.asarray(a).T)

    x = _np.asarray(x)
    given = [
        ("x", _np.concatenate([x, _np.zeros((NP - NODES, F), x.dtype)])),
        ("src", edges(src, NODES)), ("dst", edges(dst, NODES)),
        ("type8", edges(edge_type_8, 0)), ("type16", edges(edge_type_16, 0)),
        ("w_msg", rows_first(L0_gnn_message_W)), ("b_msg", _np.asarray(L0_gnn_message_b).reshape(-1)),
        ("w_ih", turned(L0_gnn_gru_w_ih)), ("w_hh", turned(L0_gnn_gru_w_hh)),
        ("b_ih", _np.asarray(L0_gnn_gru_b_ih)), ("b_hh", _np.asarray(L0_gnn_gru_b_hh)),
        ("w_l1", turned(L1_gnn_W)), ("b_l1", _np.asarray(L1_gnn_b)),
        ("w_rel", rows_first(L2_gnn_relation_weights)), ("w_self", _np.asarray(L2_gnn_self_weight)),
        ("b_l2", _np.asarray(L2_gnn_bias)), ("id_vec", _np.asarray(L3_gnn_id)),
        ("w1", _np.asarray(L3_gnn_W1)), ("b1", _np.asarray(L3_gnn_b1)), ("a1", _np.asarray(L3_gnn_a1)),
        ("w2", _np.asarray(L3_gnn_W2)), ("b2", _np.asarray(L3_gnn_b2)), ("a2", _np.asarray(L3_gnn_a2)),
    ]
    nc = _bacc.Bacc("TRN2", target_bir_lowering=False, num_devices=1)
    args = [nc.dram_tensor(f"in_{n}", a.shape, _mybir.dt.from_np(a.dtype), kind="ExternalInput").ap() for n, a in given]
    out = nc.dram_tensor("out_x", (NP, F), _mybir.dt.float32, kind="ExternalOutput").ap()
    gnn_layers(nc, *args, out)
    r = _run(nc, [{f"in_{n}": _np.ascontiguousarray(a) for n, a in given}], core_ids=[0])
    return r.results[0]["out_x"][:NODES]
```

```python
import concourse.bass as bass
from concourse import mybir
from contextlib import ExitStack

P = 128
F = 128
NODES = 12500
EDGES = 212500
TILES = -(-NODES // P)
NP = TILES * P
CH = 17
STEPS = -(-EDGES // (CH * P))
CH_LAST = -(-EDGES // P) - (STEPS - 1) * CH
W = 144
WINDOWS = -(-NP // W)
ACC = max(NP + W, WINDOWS * W)
T8, T16 = 8, 16
ROW3 = 132
HID = 256
QUAD = 4
LAG = 2
EPS = 1e-5
assert STEPS == TILES and TILES % 2 == 0


def gnn_layers(nc, x_in, src, dst, type8, type16, w_msg, b_msg, w_ih, w_hh, b_ih, b_hh, w_l1, b_l1,
               w_rel, w_self, b_l2, id_vec, w1, b1, a1, w2, b2, a2, out):
    f32, i32 = mybir.dt.float32, mybir.dt.int32
    ALU, ACT = mybir.AluOpType, mybir.ActivationFunctionType
    ds = bass.ds

    def scratch(name, shape):
        return nc.dram_tensor(name, shape, f32, kind="Internal").ap()

    tab0 = scratch("table_typed8", (NP * T8, F))
    tab2 = scratch("table_typed16", (NP * T16, F))
    tab3 = scratch("table_scaled", (NP, ROW3))
    tab4 = scratch("table_conv2", (NP, F))
    h0_d, h1_d, h2_d = (scratch(f"h{n}_rows", (NP, F)) for n in range(3))
    x1_d, x2_d, x3_d = (scratch(f"x{n}_rows", (NP, F)) for n in (1, 2, 3))
    deg_d = scratch("degree", (TILES, P))

    ctx = ExitStack()
    with ctx:
        def sb(name, shape, dt=f32):
            return ctx.enter_context(nc.sbuf_tensor(name, shape, dt))

        def pb(name, shape):
            return ctx.enter_context(nc.psum_tensor(name, shape, f32))

        ORDER = ["W", "D", "T", 0, 1, 2, 3, 4]
        ONCE = ("W", "D")
        GIVEN = {
            "h_ready": ("T", 0, 1, 2, 3), "h_transposed": ("T", 0, 1, 2, 3), "hT_ready": ("T", 0, 1, 2),
            "products": ("T", 0, 1, 2, 3, 4), "rows_ready": ("T", 1),
            "stats": ("T", 0, 1, 2), "mean_var": ("T", 0, 1, 2), "rstd": ("T", 0, 1, 2), "std": ("T", 0, 1, 2),
            "norm_ready": ("T", 0, 1, 2), "rstd_scaled": (2,),
            "slot_ready": (0, 1, 2, 3, 4), "hot_ready": (0, 1, 2, 3, 4), "sums_ready": (0, 1, 2, 3, 4),
            "sums_added": (0, 1, 2, 3, 4), "gather_go": (0, 1, 2, 3, 4), "window_ready": (0, 3),
            "aux_in": (0, 3), "weighted": (3,), "aux_added": (0, 3), "acc_zeroed": (0, 1, 2, 3, 4), "aT_ready": (0, 1, 2, 3, 4),
            "x_ready": (0, 1, 2, 4), "dinv_set": (2,),
            "rz_ready": (0,), "cand_in": (0,), "cand_ready": (0,), "r_hn": (0,), "h_less_n": (0,),
            "z_part": (0,), "gru_out": (0,),
            "mean": (1,), "mean_h": (1,), "h2_transposed": (1,), "h2T_ready": (1,), "rows_half": (1,),
            "rows_all": (1,), "rows_ready_act": (1,),
            "hid_ready": (3, 4), "conv_out": (3, 4), "below": (3, 4), "own_loop": (4,),
            "hid_transposed": (3,), "pT_ready": (3,), "products2": (3,),
            "g_slot_ready": (0, 1, 2, 3, 4),
        }
        SWEPT = {
            "g_numbered": (0, 1, 2, 3, 4), "g_hot_ready": (0, 1, 2, 3, 4), "g_sums_ready": (0, 1, 2, 3, 4),
            "g_added": (0, 1, 2, 3, 4),
        }
        SLOTS = {
            "in_loaded": {0: 2, 1: 2, 2: 2, 3: 1, 4: 2},
            "h_stored": {0: 1, 1: 1, 2: 1, 3: 1}, "x_stored": {0: 1, 1: 1, 2: 1, 4: 1},
            "rows_stored": {1: 1},
        }
        made = {}

        def total(phase, name):
            if name == "done":
                return 1
            if name in GIVEN:
                return TILES if phase in GIVEN[name] else 0
            if name in SWEPT:
                return STEPS * WINDOWS if phase in SWEPT[name] else 0
            return 16 * SLOTS[name[:-1]].get(phase, 0) * (TILES // 2)

        def S(phase, name):
            own = phase in ONCE or name[:-1] == "rows_in"
            key = (phase, name) if own else name
            if key not in made:
                made[key] = ctx.enter_context(nc.semaphore(f"{phase}_{name}" if own else name))
            return made[key]

        def at(phase, name, value):
            if phase in ONCE or name[:-1] == "rows_in" or (isinstance(value, int) and value < 1):
                return S(phase, name), value
            return S(phase, name), sum(total(q, name) for q in ORDER[2:ORDER.index(phase)]) + value

        def after(eng, sem, value):
            if isinstance(value, int) and value < 1:
                return
            eng.wait_ge(sem, value)

        def hold(eng, name):
            eng.sem_inc(S("W", f"{name}_held"), 1)

        acc = sb("acc", [P, ACC])
        aux = sb("aux", [1, ACC])
        src_sb = sb("src_sb", [P, STEPS * CH], i32)
        dst_sb = sb("dst_sb", [P, STEPS * CH], i32)
        typed = sb("typed", [P, STEPS * CH], i32)
        rel = dst_sb[:, :].bitcast(f32)
        base_i = sb("base_i", [1, STEPS], i32)
        slot = [sb(f"slot{k}", [P, CH], i32) for k in range(2)]
        rows = [sb(f"rows{k}", [P, CH, ROW3]) for k in range(2)]
        hot = [sb(f"hot{k}", [P, CH, W]) for k in range(2)]
        hot_sum = [sb(f"hot_sum{k}", [P, W]) for k in range(2)]
        node_i = sb("node_i", [P, W], i32)
        node = sb("node", [P, W])
        ident = sb("ident", [P, P])
        ones = sb("ones", [P, P])
        zero = sb("zero", [P, P])
        base_all = sb("base_all", [P, STEPS])
        node_w = sb("node_w", [P, W])
        bad_sb = sb("bad_sb", [P, 3])
        extreme = sb("extreme", [P, 4])
        ahead = sb("ahead", [1, STEPS])
        disorder_sb = sb("disorder_sb", [1, 1], i32)
        base_f = sb("base_f", [1, STEPS])
        wih_sb = sb("wih_sb", [P, 3 * F])
        whh_sb = sb("whh_sb", [P, 3 * F])
        bg_sb = sb("bg_sb", [1, 4 * F])
        bh_sb = sb("bh_sb", [1, 2 * F])
        wl1_sb = sb("wl1_sb", [P, F])
        bl1_sb = sb("bl1_sb", [1, F])
        wrel_sb = sb("wrel_sb", [P, T16 * F])
        wself_sb = sb("wself_sb", [P, F])
        bl2_sb = sb("bl2_sb", [1, F])
        id_sb = sb("id_sb", [8, 1])
        w1b_sb = sb("w1b_sb", [8, HID])
        idw_sb = sb("idw_sb", [1, HID])
        deg_t = sb("deg_t", [TILES, P])
        rdeg = sb("rdeg", [P, TILES])
        dinv = sb("dinv", [P, TILES])
        degm = sb("degm", [P, TILES])
        root = sb("root", [P, TILES])
        x_t = [sb(f"x_t{k}", [P, F]) for k in range(2)]
        h_t = [sb(f"h_t{k}", [P, ROW3]) for k in range(2)]
        xo_t = [sb(f"xo_t{k}", [P, F]) for k in range(2)]
        ho_t = [sb(f"ho_t{k}", [P, ROW3]) for k in range(2)]
        big_t = [sb(f"big_t{k}", [P, T16 * F]) for k in range(2)]
        h_quad = hot[0][:, :, :].rearrange("p c w -> p (c w)")[:, 0:QUAD * F].rearrange("p (k f) -> p k f", f=F)
        rows8 = [big_t[k % 2][:, (k // 2) * T8 * F:(k // 2 + 1) * T8 * F] for k in range(QUAD)]
        wmsg_sb, bmsg_sb = (rows[k][:, :, :].rearrange("p c r -> p (c r)")[:, 0:T8 * F] for k in range(2))
        w1a_sb, b1_sb, a1_sb = (big_t[1][:, n * HID:(n + 1) * HID] for n in range(3))
        w2_sb = big_t[1][:, 3 * HID:4 * HID].rearrange("p (k f) -> p k f", k=2)
        b2_sb, a2_sb = (big_t[1][:, 4 * HID + n * F:4 * HID + (n + 1) * F] for n in range(2))
        hid_a, hid_b, hid_c, pT = (big_t[0][:, n * HID:(n + 1) * HID] for n in range(4))
        hT = [sb(f"hT{k}", [P, P]) for k in range(2)]
        h2T = sb("h2T", [P, P])
        aT = sb("aT", [P, P])
        aux_t = sb("aux_t", [1, P])
        rz = sb("rz", [P, 2 * F])
        gate_a, gate_b, cand = (sb(n, [P, F]) for n in ("gate_a", "gate_b", "cand"))
        stats = [sb(f"stats{k}", [P, 6]) for k in range(2)]
        mv = [sb(f"mv{k}", [P, 2]) for k in range(2)]
        std = [sb(f"std{k}", [P, 1]) for k in range(2)]
        eps = sb("eps", [P, 1])
        rstd = [sb(f"rstd{k}", [P, 1]) for k in range(2)]
        nmr = [sb(f"nmr{k}", [P, 1]) for k in range(2)]

        big = pb("big", [P, 4 * 512])
        win = [pb(f"win{k}", [P, 512]) for k in range(2)]
        auxp = pb("auxp", [P, 512])
        trp = pb("trp", [P, 512])

        TABLE = [tab0, h1_d, tab2, tab3, tab4]
        INDEX = [typed, src_sb, typed, src_sb, src_sb]
        WIDTH = [F, F, F, ROW3, F]
        X_IN = [x_in, x1_d, x2_d, None, x3_d]
        H_IN = [h0_d, h1_d, h2_d, tab3, tab4]
        X_OUT = [x1_d, x2_d, x3_d, None, out]
        H_OUT = [h1_d, h2_d, tab3, tab4, None]
        AX = mybir.AxisListType
        AUX = (0, 3)

        def turns(eng, *stages, closing=None, ring=2):
            ahead = -min(0, *[lag for lag, _ in stages])
            behind = max(0, *[lag for lag, _ in stages])
            first = -(-(behind + ring) // ring)
            last = (TILES - 1 - ahead) // ring

            def peeled(start, end):
                for s in range(start, end):
                    for lag, stage in closing if closing and s >= STEPS - 2 else stages:
                        if 0 <= s - lag < TILES:
                            stage(s - lag, (s - lag) // ring, (s - lag) % ring)

            peeled(-ahead, ring * first)
            with eng.Fori(first, last) as i:
                for k in range(ring):
                    for lag, stage in stages:
                        stage(ring * i + (k - lag), i + (k - lag) // ring, (k - lag) % ring)
            peeled(ring * last, TILES + behind)

        def all_tiles(eng, *stages):
            for t in range(2):
                for stage in stages:
                    stage(t, 0, t)
            with eng.Fori(1, TILES // 2) as i:
                for k in range(2):
                    for stage in stages:
                        stage(2 * i + k, i, k)

        def chunks(t):
            return CH_LAST if isinstance(t, int) and t == STEPS - 1 else CH

        def last_steps(p, t):
            return p == 3 and isinstance(t, int) and t >= STEPS - 2

        def by_order(eng, layers):
            eng.wait_ge(*at("W", "disorder", 1))
            disorder = eng.value_load(disorder_sb[0:1, 0:1], min_val=0, max_val=1)
            with eng.If(disorder == 0):
                layers(False)
            with eng.Else():
                layers(True)

        def tile_rows(ap, t):
            return ap[ds(t * P, P), :]

        def tile_cols(t):
            return acc[:, ds(t * P, P)]

        def tiles_rows(ap, t, tiles):
            return ap[ds(t * P, tiles * P), :].rearrange("(t p) f -> p t f", p=P)

        def tiles_cols(t, tiles):
            return acc[:, ds(t * P, tiles * P)].rearrange("p (t f) -> p t f", f=P)

        def by_quads(stage):
            def run(t, i, k):
                whole = not isinstance(t, int) or t < TILES // QUAD * QUAD
                stage(t, i, k, QUAD if whole else TILES % QUAD)
            return run

        def typed_rows(ap, t, n):
            return ap[ds(t * (P * n), P * n), :].rearrange("(p r) f -> p (r f)", r=n)

        block = ctx.enter_context(nc.Block())

        @block.sync
        def _(sp):
            def load_quad(t, i, k, tiles=QUAD):
                if k == 0:
                    after(sp, *at("T", "quad_loaded", 16 * i))
                    hold(sp, "sp")
                    sp.dma_start(tiles_cols(t, tiles), tiles_rows(x_in, t, tiles)).then_inc(S("T", "quad_loaded"), 16)

            def store_pair(t, i, k):
                if k % 2 == 1:
                    sp.wait_ge(*at("T", "h_ready", t + 1))
                    hold(sp, "sp")
                    sp.dma_start(tiles_rows(h0_d, t - 1, 2), h_quad[:, k - 1:k + 1, :]).then_inc(S("T", f"pair_stored{k // 2}"), 16)

            def store_rows(t, i, k):
                sp.wait_ge(*at("T", "rows_ready", t + 1))
                hold(sp, "sp")
                sp.dma_start(typed_rows(tab0, t, T8), rows8[k]).then_inc(S("T", f"typed_stored{k}"), 16)

            def load_edges(t, i, k):
                if isinstance(t, int) and t == QUAD:
                    sp.dma_start(dst_sb[:, :], dst).then_inc(S("W", "edges"), 16)
                    sp.dma_start(src_sb[:, :], src).then_inc(S("W", "edges"), 16)
                    sp.dma_start(typed[:, :], type8).then_inc(S("W", "edges"), 16)

            turns(sp, (-QUAD, by_quads(load_quad)), (0, load_edges), (4, store_rows), (0, store_pair), ring=QUAD)
            for k in range(2):
                sp.wait_ge(*at("T", f"pair_stored{k}", 16 * len(range(2 * k, TILES, QUAD))))
            for k in range(QUAD):
                sp.wait_ge(*at("T", f"typed_stored{k}", 16 * len(range(k, TILES, QUAD))))
            sp.sem_inc(S("T", "done"), 1)

            def load(p, t, i, k):
                after(sp, *at(p, "x_ready" if p != 3 else "h_transposed", t - 1))
                hold(sp, "sp")
                if X_IN[p] is not None:
                    sp.dma_start(x_t[k][:, :], tile_rows(X_IN[p], t)).then_inc(S(p, f"in_loaded{k}"), 16)
                hw = H_IN[p].shape[1]
                sp.dma_start(h_t[k][:, 0:hw], tile_rows(H_IN[p], t)).then_inc(S(p, f"in_loaded{k}"), 16)

            def store(p, t, i, k):
                if X_OUT[p] is not None:
                    sp.wait_ge(*at(p, "x_ready", t + 1))
                    hold(sp, "sp")
                    sp.dma_start(tile_rows(X_OUT[p], t), xo_t[k][:, :]).then_inc(S(p, f"x_stored{k}"), 16)
                if H_OUT[p] is not None:
                    hw = H_OUT[p].shape[1]
                    sp.wait_ge(*at(p, "h_ready", t + 1))
                    hold(sp, "sp")
                    if p == 2:
                        sp.wait_ge(*at(p, "dinv_set", t + 1))
                        hold(sp, "sp")
                    sp.dma_start(tile_rows(H_OUT[p], t), ho_t[k][:, 0:hw]).then_inc(S(p, f"h_stored{k}"), 16)

            def store_typed(p, t, i, k):
                if p == 1:
                    sp.wait_ge(*at(p, "rows_ready", t + 1))
                    hold(sp, "sp")
                    sp.wait_ge(*at(p, "rows_ready_act", t + 1))
                    hold(sp, "sp")
                    sp.dma_start(typed_rows(tab2, t, T16), big_t[k][:, :]).then_inc(S(p, f"rows_stored{k}"), 16)

            def layers(general):
                for p in range(5):
                    if p == 1:
                        sp.dma_start(typed[:, :], type16).then_inc(S("W", "type16"), 16)
                        sp.dma_start(deg_d.rearrange("(o t) p -> o (t p)", o=1), aux[0:1, 0:NP]).then_inc(S("D", "deg_out"), 16)
                        sp.wait_ge(*at("D", "deg_out", 16))
                        sp.dma_start(deg_t[:, :], deg_d).then_inc(S("D", "deg_in"), 16)

                    def load_p(t, i, k, p=p):
                        load(p, t, i, k)

                    def store_p(t, i, k, p=p):
                        store(p, t, i, k)

                    def store_typed_p(t, i, k, p=p):
                        store_typed(p, t, i, k)

                    if general:
                        all_tiles(sp, load_p, store_p, store_typed_p)
                    else:
                        turns(sp, (1, load_p), (LAG, store_p), (LAG + 1, store_typed_p))
                    for k in range(2):
                        for name, used in (("x", X_OUT[p] is not None), ("h", H_OUT[p] is not None), ("rows", p == 1)):
                            if used:
                                sp.wait_ge(*at(p, f"{name}_stored{k}", 16 * (TILES // 2)))
                    sp.sem_inc(S(p, "done"), 1)

            by_order(sp, layers)

        @block.gpsimd
        def _(pool):
            pool.iota(node_i[:, :], [[1, W]], base=0, channel_multiplier=0).then_inc(S("W", "node_i"), 1)
            pool.memset(zero[:, :], 0.0)
            pool.memset(ones[:, :], 1.0).then_inc(S("W", "ones"), 1)
            pool.memset(eps[:, :], EPS).then_inc(S("W", "eps"), 1)
            pool.memset(ident[:, :], 0.0).then_inc(S("W", "zeroed"), 1)
            pool.wait_ge(*at("W", "zeroed", 1))
            pool.affine_select(out=ident[:, :], in_=ident[:, :], compare_op=ALU.not_equal, fill=1.0, base=0,
                               pattern=[[-1, P]], channel_multiplier=1).then_inc(S("W", "ident"), 1)
            pool.memset(aux[:, :], 0.0).then_inc(S("W", "aux_zero"), 1)

            def load(dst_ap, src_ap, group):
                pool.dma_start(dst_ap, src_ap).then_inc(S("W", group), 16)

            def spread(vec):
                return vec.rearrange("(o n) -> o n", o=1)

            load(bg_sb[:, 0:3 * F], spread(b_ih), "gru")
            load(bg_sb[:, 3 * F:4 * F], spread(b_hh)[:, 2 * F:3 * F], "gru")
            load(bh_sb[:, :], spread(b_hh)[:, 0:2 * F], "gru")
            load(wih_sb[:, :], w_ih, "gru")
            load(whh_sb[:, :], w_hh, "gru")
            load(wl1_sb[:, :], w_l1, "rest")
            load(bl1_sb[:, :], spread(b_l1), "rest")
            load(wrel_sb[:, :], w_rel, "rest")
            load(wself_sb[:, :], w_self, "rest")
            load(bl2_sb[:, :], spread(b_l2), "rest")
            load(id_sb[:, :], id_vec.rearrange("(n o) -> n o", o=1), "rest")
            load(w1b_sb[:, :], w1[F:F + 8, :], "rest")

            def gather(p, k, n, signal):
                for c in range(n):
                    pool.indirect_dma_start(
                        rows[k][:, c, 0:WIDTH[p]], None, TABLE[p],
                        bass.IndirectOffsetOnAxis(ap=slot[k][:, c:c + 1], axis=0),
                    ).then_inc(S(p, signal), 16)

            def layers(general):
                for p in range(5):
                    pool.wait_ge(*at("T" if p == 0 else p - 1, "done", 1))

                    def agg(t, i, k, p=p):
                        pool.wait_ge(*at(p, "slot_ready", t + 1))
                        after(pool, *at(p, "weighted" if p == 3 else "sums_ready", t - 1))
                        hold(pool, "pool")
                        gather(p, k, chunks(t), f"rows_in{k}")

                    def sweep(s, p=p):
                        pool.wait_ge(*at(p, "g_slot_ready", s + 1))
                        after(pool, *at(p, "g_added", WINDOWS * s))
                        hold(pool, "pool")
                        gather(p, 0, CH, "rows_in2")

                    if general:
                        sweep(0)
                        with pool.Fori(1, STEPS) as s:
                            sweep(s)
                    else:
                        turns(pool, (0, agg))

            by_order(pool, layers)

        @block.scalar
        def _(act):
            def load(dst_ap, src_ap, group):
                act.dma_start(dst_ap, src_ap).then_inc(S("W", group), 16)

            load(wmsg_sb, w_msg, "msg")
            load(bmsg_sb, b_msg.partition_broadcast(P), "msg")

            def deviation(ph, t, k):
                act.wait_ge(*at(ph, "mean_var", t + 1))
                act.activation(std[k][:, :], mv[k][:, 1:2], ACT.Sqrt, bias=eps[:, 0:1]).then_inc(S(ph, "std"), 1)

            def normalise(ph, t, k, x_ap, h_ap):
                act.wait_ge(*at(ph, "norm_ready", t + 1))
                act.activation(h_ap, x_ap, ACT.Relu, bias=nmr[k][:, 0:1], scale=rstd[k][:, 0:1]).then_inc(S(ph, "h_ready"), 1)

            def deviation_first(t, i, k):
                deviation("T", t, k % 2)

            def norm_first(t, i, k):
                after(act, *at("T", f"pair_stored{k // 2}", 16 * i))
                after(act, *at("T", "h_transposed", t - 3))
                normalise("T", t, k % 2, tile_cols(t), h_quad[:, k, :])

            def copy_first(t, i, k):
                act.wait_ge(*at("T", "h_transposed", t + 1))
                after(act, *at("T", "products", t - 1))
                act.copy(hT[k % 2][:, :], win[k % 2][:, 0:P]).then_inc(S("T", "hT_ready"), 1)

            act.wait_ge(*at("W", "eps", 1))
            turns(act, (0, deviation_first), (2, copy_first), (0, norm_first), ring=QUAD)

            def layers(general):
                for p in range(5):
                    def agg(t, i, k, p=p):
                        after(act, *at(p, f"rows_in{k}", 16 * CH * i))
                        act.copy(slot[k][:, :], INDEX[p][:, ds(t * CH, CH)]).then_inc(S(p, "slot_ready"), 1)

                    def dense(t, i, k, p=p):
                        if p in (0, 1, 2):
                            act.wait_ge(*at(p, "h_transposed", t + 1))
                            act.copy(hT[0][:, :], trp[:, 0:P]).then_inc(S(p, "hT_ready"), 1)
                        if p == 0:
                            act.wait_ge(*at(p, "products", t + 1))
                            act.activation(rz[:, :], big[:, 0:2 * F], ACT.Sigmoid).then_inc(S(p, "rz_ready"), 1)
                            act.wait_ge(*at(p, "cand_in", t + 1))
                            act.activation(cand[:, :], gate_b[:, :], ACT.Tanh).then_inc(S(p, "cand_ready"), 1)
                        if p in (0, 1, 2):
                            after(act, *at(p, f"h_stored{k}", 16 * i))
                            deviation(p, t, k)
                            normalise(p, t, k, xo_t[k][:, :], ho_t[k][:, 0:F])
                        if p == 1:
                            act.wait_ge(*at(p, "h2_transposed", t + 1))
                            act.copy(h2T[:, :], trp[:, 0:P]).then_inc(S(p, "h2T_ready"), 1)
                        if p == 3:
                            act.wait_ge(*at(p, "hid_transposed", t + 1))
                            act.copy(pT, trp[:, 0:HID]).then_inc(S(p, "pT_ready"), 1)
                            act.wait_ge(*at(p, "products2", t + 1))
                            after(act, *at(p, f"h_stored{k}", 16 * i))
                            act.activation(ho_t[k][:, 0:F], big[:, 512:512 + F], ACT.Identity,
                                           scale=dinv[:, ds(t, 1)]).then_inc(S(p, "h_ready"), 1)

                    def typed_out(t, i, k, p=p):
                        after(act, *at(p, f"rows_stored{k}", 16 * i))
                        act.wait_ge(*at(p, "rows_half", t + 1))
                        act.copy(big_t[k][:, 0:8 * F], big[:, 0:8 * F]).then_inc(S(p, "rows_ready_act"), 1)

                    def once(t, i, k, p=p):
                        if isinstance(t, int) and t == 0:
                            if p == 1:
                                act.wait_ge(*at("D", "degm", 1))
                                act.activation(root[:, :], trp[:, 0:TILES], ACT.Sqrt, bias=ones[:, 0:1])\
                                    .then_inc(S("D", "root"), 1)
                            if p == 2:
                                load(w1a_sb, w1[0:F, :], "late")
                                load(b1_sb, b1.partition_broadcast(P), "late")
                                load(a1_sb, a1.partition_broadcast(P), "late")
                                load(w2_sb, w2.rearrange("(k p) f -> p k f", k=2), "late")
                                load(b2_sb, b2.partition_broadcast(P), "late")
                                load(a2_sb, a2.partition_broadcast(P), "late")

                    act.wait_ge(*at("T" if p == 0 else p - 1, "done", 1))
                    if p == 0:
                        act.wait_ge(*at("W", "idx8", 1))
                    if p == 2:
                        act.wait_ge(*at("W", "idx16", 1))

                    def sweep(s, p=p):
                        after(act, *at(p, "rows_in2", 16 * CH * s))
                        act.copy(slot[0][:, :], INDEX[p][:, ds(s * CH, CH)]).then_inc(S(p, "g_slot_ready"), 1)

                    out_stage = [(LAG + 1, typed_out)] if p == 1 else []
                    if general:
                        sweep(0)
                        once(0, 0, 0)
                        with act.Fori(1, STEPS) as s:
                            sweep(s)
                        all_tiles(act, dense, *[stage for _, stage in out_stage])
                    else:
                        turns(act, (-1, agg), (0, once), (LAG, dense), *out_stage)

            by_order(act, layers)

        @block.tensor
        def _(pe):
            mm = nc.tensor.matmul
            pe.wait_ge(*at("W", "ones", 1))
            pe.wait_ge(*at("W", "ident", 1))
            pe.wait_ge(*at("W", "msg", 32))

            def transpose_first(t, i, k):
                pe.wait_ge(*at("T", "h_ready", t + 1))
                after(pe, *at("T", "hT_ready", t - 1))
                nc.tensor.transpose(win[k % 2][:, 0:P], h_quad[:, k, :], ident[:, :]).then_inc(S("T", "h_transposed"), 1)

            def products_first(t, i, k):
                pe.wait_ge(*at("T", "hT_ready", t + 1))
                after(pe, *at("T", "rows_ready", t - 1))
                for j in range(2):
                    last_mm = mm(big[:, (2 * (k % 2) + j) * 512:(2 * (k % 2) + j + 1) * 512], hT[k % 2][:, :],
                                 wmsg_sb[:, j * 512:(j + 1) * 512], start=True, stop=True)
                last_mm.then_inc(S("T", "products"), 1)

            turns(pe, (2, transpose_first), (3, products_first), ring=QUAD)

            pe.wait_ge(*at("W", "base_f", 1))
            mm(auxp[:, 0:STEPS], ones[0:1, :], base_f[:, :], start=True, stop=True).then_inc(S("W", "base_all"), 1)
            pe.wait_ge(*at("W", "bad", 3))
            mm(trp[0:1, 0:3], ones[:, 0:1], bad_sb[:, :], start=True, stop=True).then_inc(S("W", "bad_sum"), 1)
            pe.wait_ge(*at("W", "disorder", 1))

            pe.wait_ge(*at("W", "gru", 16 * 5))
            pe.wait_ge(*at("W", "bg", 1))
            pe.wait_ge(*at("W", "rest", 16 * 7))
            pe.wait_ge(*at("W", "rel", 1))
            mm(auxp[0:1, 0:HID], id_sb[:, :], w1b_sb[:, :], start=True, stop=True).then_inc(S("W", "idw_mm"), 1)
            pe.wait_ge(*at("W", "idw", 1))

            def layers(general):
                for p in range(5):
                    pe.wait_ge(*at("T" if p == 0 else p - 1, "done", 1))
                    if p == 3:
                        pe.wait_ge(*at("W", "late", 16 * 6))
                    if p == 1:
                        pe.wait_ge(*at("D", "deg_in", 16))
                        nc.tensor.transpose(trp[:, 0:TILES], deg_t[:, :], ident[0:TILES, 0:TILES]).then_inc(S("D", "deg_cols"), 1)
                        pe.wait_ge(*at("D", "deg_done", 1))

                    def add_up(target, values, hots, n, first, end):
                        for c in range(first, end):
                            last_mm = mm(target, values(c), hots[:, c, :], start=c == 0, stop=c == n - 1)
                        return last_mm

                    def row(k, p=p):
                        return lambda c: rows[k][:, c, 0:F]

                    def weight(k, p=p):
                        return lambda c: ones[:, 0:1] if p == 0 else rows[k][:, c, F:F + 1]

                    def sums_begin(t, i, k, p=p):
                        pe.wait_ge(*at(p, f"rows_in{k}", 16 * CH * i + 16 * chunks(t)))
                        pe.wait_ge(*at(p, "hot_ready", t + 1))
                        after(pe, *at(p, "sums_added", t - 1))
                        add_up(win[k][:, 0:W], row(k), hot[k], chunks(t), 0, CH // 2)

                    def sums_end(t, i, k, p=p):
                        add_up(win[k][:, 0:W], row(k), hot[k], chunks(t), CH // 2, chunks(t))\
                            .then_inc(S(p, "window_ready" if p in AUX else "sums_ready"), 1)

                    def aux_sums(t, i, k, p=p):
                        after(pe, *at(p, "aux_added", t))
                        if last_steps(p, t):
                            add_up(auxp[0:1, 0:W], weight(k), hot[k], chunks(t), 0, chunks(t)).then_inc(S(p, "sums_ready"), 1)
                        else:
                            pe.wait_ge(*at(p, "aux_in", t + 1))
                            mm(auxp[0:1, 0:W], ones[:, 0:1], hot_sum[k][:, :], start=True, stop=True)\
                                .then_inc(S(p, "sums_ready"), 1)

                    def sweep(s, p=p):
                        pe.wait_ge(*at(p, "rows_in2", 16 * CH * (s + 1)))
                        hold(pe, "pe")
                        with pe.Fori(0, WINDOWS) as w:
                            pe.wait_ge(*at(p, "g_hot_ready", s * WINDOWS + w + 1))
                            if p in AUX:
                                add_up(auxp[0:1, 0:W], weight(0), hot[0], CH, 0, CH)
                            add_up(win[0][:, 0:W], row(0), hot[0], CH, 0, CH).then_inc(S(p, "g_sums_ready"), 1)

                    def transpose_in(t, i, k, p=p):
                        if p != 4:
                            n_in = 1 if X_IN[p] is None else 2
                            pe.wait_ge(*at(p, f"in_loaded{k}", 16 * n_in * (i + 1)))
                            if p == 1:
                                after(pe, *at(p, "h2T_ready", t))
                            last_mm = nc.tensor.transpose(trp[:, 0:P], h_t[k][:, 0:F], ident[:, :])
                            if p == 3:
                                last_mm = nc.tensor.transpose(trp[0:1, P:2 * P], h_t[k][:, F:F + 1], ident[:, :])
                            last_mm.then_inc(S(p, "h_transposed"), 1)

                    def products(t, i, k, p=p):
                        pe.wait_ge(*at(p, "aT_ready", t + 1))
                        if p == 0:
                            mm(big[:, 0:4 * F], ones[0:1, :], bg_sb[:, :], start=True, stop=False)
                            mm(big[:, 0:3 * F], aT[:, :], wih_sb[:, :], start=False, stop=False)
                            pe.wait_ge(*at(p, "hT_ready", t + 1))
                            mm(big[:, 0:2 * F], hT[0][:, :], whh_sb[:, 0:2 * F], start=False, stop=False)
                            mm(big[:, 3 * F:4 * F], hT[0][:, :], whh_sb[:, 2 * F:3 * F], start=False, stop=True)\
                                .then_inc(S(p, "products"), 1)
                        if p == 1:
                            mm(auxp[:, 0:F], aT[:, :], wl1_sb[:, :], start=True, stop=True)
                            mm(auxp[:, F:2 * F], ones[0:1, :], bl1_sb[:, :], start=True, stop=False)
                            pe.wait_ge(*at(p, "hT_ready", t + 1))
                            mm(auxp[:, F:2 * F], hT[0][:, :], wl1_sb[:, :], start=False, stop=True)\
                                .then_inc(S(p, "products"), 1)
                        if p == 2:
                            mm(big[:, 0:F], ones[0:1, :], bl2_sb[:, :], start=True, stop=False)
                            mm(big[:, 0:F], aT[:, :], ident[:, :], start=False, stop=False)
                            pe.wait_ge(*at(p, "hT_ready", t + 1))
                            mm(big[:, 0:F], hT[0][:, :], wself_sb[:, :], start=False, stop=True).then_inc(S(p, "products"), 1)
                        if p == 3:
                            mm(big[:, 0:HID], aT[:, :], w1a_sb, start=True, stop=False)
                            mm(big[:, 0:HID], aux_t[:, :], idw_sb[:, :], start=False, stop=True).then_inc(S(p, "products"), 1)
                        if p == 4:
                            nc.tensor.transpose(big[:, 0:F], aT[:, :], ident[:, :]).then_inc(S(p, "products"), 1)

                    def transpose_out(t, i, k, p=p):
                        if p == 1:
                            pe.wait_ge(*at(p, "h_ready", t + 1))
                            nc.tensor.transpose(trp[:, 0:P], ho_t[k][:, 0:F], ident[:, :]).then_inc(S(p, "h2_transposed"), 1)
                        if p == 3:
                            pe.wait_ge(*at(p, "hid_ready", t + 1))
                            for j in range(2):
                                last_mm = nc.tensor.transpose(trp[:, j * P:(j + 1) * P], hid_c[:, j * P:(j + 1) * P], ident[:, :])
                            last_mm.then_inc(S(p, "hid_transposed"), 1)

                    def products_out(t, i, k, p=p):
                        if p == 1:
                            pe.wait_ge(*at(p, "h2T_ready", t + 1))
                            after(pe, *at(p, "rows_ready_act", t))
                            after(pe, *at(p, "rows_ready", t))
                            for j in range(4):
                                last_mm = mm(big[:, j * 512:(j + 1) * 512], h2T[:, :], wrel_sb[:, j * 512:(j + 1) * 512],
                                             start=True, stop=True)
                                if j == 1:
                                    last_mm.then_inc(S(p, "rows_half"), 1)
                            last_mm.then_inc(S(p, "rows_all"), 1)
                        if p == 3:
                            pe.wait_ge(*at(p, "pT_ready", t + 1))
                            for j in range(2):
                                last_mm = mm(big[:, 512:512 + F], pT[:, j * P:(j + 1) * P], w2_sb[:, j, :],
                                             start=j == 0, stop=j == 1)
                            last_mm.then_inc(S(p, "products2"), 1)

                    def dense(t, i, k, p=p):
                        for part in (transpose_in, products, transpose_out) + (products_out,) * (p != 1):
                            part(t, i, k)

                    sums = [(0, sums_begin), (0, sums_end)] + [(0, aux_sums)] * (p in AUX)

                    if general:
                        with pe.Fori(0, STEPS) as s:
                            sweep(s)
                        all_tiles(pe, dense, *[products_out] * (p == 1))
                    elif p == 1:
                        turns(pe, (LAG, transpose_in), (0, sums_begin), (LAG, products), (0, sums_end),
                              (LAG + 1, products_out), (LAG, transpose_out),
                              closing=[(LAG, transpose_in), (LAG, products), (LAG + 1, products_out),
                                       (LAG, transpose_out)] + sums)
                    else:
                        turns(pe, (LAG, transpose_in), (0, sums_begin), (LAG, products), (0, sums_end),
                              (LAG, transpose_out), (LAG, products_out), *[(0, aux_sums)] * (p in AUX),
                              closing=[(LAG, dense)] + sums)

            by_order(pe, layers)

        @block.vector
        def _(dve):
            V = nc.vector
            dve.wait_ge(*at("W", "node_i", 1))
            V.tensor_copy(node[:, :], node_i[:, :]).then_inc(S("W", "node"), 1)

            def moments(ph, t, k, x_ap):
                V.bn_stats(stats[k][:, :], x_ap).then_inc(S(ph, "stats"), 1)
                dve.wait_ge(*at(ph, "stats", t + 1))
                hold(dve, "dve")
                V.bn_aggr(mv[k][:, :], stats[k][:, :]).then_inc(S(ph, "mean_var"), 1)

            def normalise(ph, t, k, scale=None):
                dve.wait_ge(*at(ph, "std", t + 1))
                V.reciprocal(rstd[k][:, :], std[k][:, :]).then_inc(S(ph, "rstd"), 1)
                dve.wait_ge(*at(ph, "rstd", t + 1))
                if scale is not None:
                    V.tensor_scalar(rstd[k][:, :], rstd[k][:, :], scale, None, ALU.mult).then_inc(S(ph, "rstd_scaled"), 1)
                    dve.wait_ge(*at(ph, "rstd_scaled", t + 1))
                V.scalar_tensor_tensor(out=nmr[k][:, :], in0=mv[k][:, 0:1], scalar=-1.0, in1=rstd[k][:, :],
                                       op0=ALU.mult, op1=ALU.mult).then_inc(S(ph, "norm_ready"), 1)

            def moments_first(t, i, k):
                if k == 0:
                    dve.wait_ge(*at("T", "quad_loaded", 16 * (i + 1)))
                after(dve, *at("T", "h_ready", t - 1))
                moments("T", t, k % 2, tile_cols(t))

            def rows_first(t, i, k):
                if isinstance(t, int) and t == 0:
                    dve.wait_ge(*at("W", "msg", 32))
                dve.wait_ge(*at("T", "products", t + 1))
                after(dve, *at("T", f"typed_stored{k}", 16 * i))
                V.tensor_tensor(rows8[k], big[:, (k % 2) * 1024:(k % 2 + 1) * 1024], bmsg_sb, ALU.add)\
                    .then_inc(S("T", "rows_ready"), 1)

            turns(dve, (0, moments_first), (4, rows_first), (0, lambda t, i, k: normalise("T", t, k % 2)), ring=QUAD)
            dve.wait_ge(*at("W", "edges", 48))
            V.tensor_copy(base_i[:, :], dst_sb[0:1, :].rearrange("o (s c) -> o s c", c=CH)[:, :, 0])
            V.tensor_copy(base_f[:, :], dst_sb[0:1, :].rearrange("o (s c) -> o s c", c=CH)[:, :, 0]).then_inc(S("W", "base_f"), 1)
            V.scalar_tensor_tensor(out=typed[:, :], in0=src_sb[:, :], scalar=float(T8), in1=typed[:, :],
                                   op0=ALU.mult, op1=ALU.add).then_inc(S("W", "idx8"), 1)
            dve.wait_ge(*at("W", "base_all", 1))
            V.tensor_tensor(rel.rearrange("p (s c) -> p s c", c=CH), dst_sb[:, :].rearrange("p (s c) -> p s c", c=CH),
                            auxp[:, 0:STEPS].unsqueeze(2).to_broadcast([P, STEPS, CH]), ALU.subtract).then_inc(S("W", "rel"), 1)
            V.memset(bad_sb[:, :], 0.0).then_inc(S("W", "bad_zero"), 1)
            V.tensor_copy(base_all[:, :], auxp[:, 0:STEPS])
            dve.wait_ge(*at("W", "rel", 1))
            V.tensor_reduce(extreme[:, 0:1], rel[:, 0:(STEPS - 1) * CH + CH_LAST], AX.X, ALU.max)
            V.tensor_reduce(extreme[:, 1:2], rel[:, 0:(STEPS - 1) * CH + CH_LAST], AX.X, ALU.min).then_inc(S("W", "extreme"), 1)
            dve.wait_ge(*at("W", "node", 1))
            V.scalar_tensor_tensor(out=ahead[:, :], in0=node[0:1, 0:STEPS], scalar=-float(P), in1=base_f[:, :],
                                   op0=ALU.mult, op1=ALU.add).then_inc(S("W", "ahead"), 1)
            dve.wait_ge(*at("W", "ahead", 1))
            V.tensor_reduce(extreme[0:1, 2:3], ahead[:, :], AX.X, ALU.min).then_inc(S("W", "extreme"), 1)
            dve.wait_ge(*at("W", "extreme", 2))
            dve.wait_ge(*at("W", "bad_zero", 1))
            V.tensor_scalar(bad_sb[:, 0:1], extreme[:, 0:1], float(W), None, ALU.is_ge).then_inc(S("W", "bad"), 1)
            V.tensor_scalar(bad_sb[:, 1:2], extreme[:, 1:2], 0.0, None, ALU.is_lt).then_inc(S("W", "bad"), 1)
            V.tensor_scalar(bad_sb[0:1, 2:3], extreme[0:1, 2:3], -float(P), None, ALU.is_lt).then_inc(S("W", "bad"), 1)
            dve.wait_ge(*at("W", "bad_sum", 1))
            V.tensor_reduce(extreme[0:1, 3:4], trp[0:1, 0:3], AX.X, ALU.add).then_inc(S("W", "bad_total"), 1)
            dve.wait_ge(*at("W", "bad_total", 1))
            V.tensor_scalar(disorder_sb[:, :], extreme[0:1, 3:4], 1.0, None, ALU.min).then_inc(S("W", "disorder"), 1)
            dve.wait_ge(*at("W", "gru", 16 * 5))
            V.tensor_tensor(bg_sb[:, 0:2 * F], bg_sb[:, 0:2 * F], bh_sb[:, :], ALU.add).then_inc(S("W", "bg"), 1)
            dve.wait_ge(*at("W", "idw_mm", 1))
            V.tensor_copy(idw_sb[:, :], auxp[0:1, 0:HID]).then_inc(S("W", "idw"), 1)
            dve.wait_ge(*at("W", "node", 1))
            dve.wait_ge(*at("W", "rest", 16 * 7))

            def layers(general):
                for p in range(5):
                    dve.wait_ge(*at("T" if p == 0 else p - 1, "done", 1))
                    if p == 1:
                        dve.wait_ge(*at("W", "type16", 16))
                        V.scalar_tensor_tensor(out=typed[:, :], in0=src_sb[:, :], scalar=float(T16), in1=typed[:, :],
                                               op0=ALU.mult, op1=ALU.add).then_inc(S("W", "idx16"), 1)
                        dve.wait_ge(*at("D", "deg_cols", 1))
                        V.tensor_scalar(degm[:, :], trp[:, 0:TILES], 1.0, None, ALU.max).then_inc(S("D", "degm"), 1)
                        dve.wait_ge(*at("D", "root", 1))
                        V.reciprocal(dinv[:, :], root[:, :])
                        dve.wait_ge(*at("D", "degm", 1))
                        V.reciprocal(rdeg[:, :], degm[:, :]).then_inc(S("D", "deg_done"), 1)
                        dve.wait_ge(*at("D", "deg_done", 1))
                    if p == 3:
                        dve.wait_ge(*at("W", "late", 16 * 6))
                    if p == 0:
                        dve.wait_ge(*at("W", "aux_zero", 1))
                        V.memset(acc[:, :], 0.0).then_inc(S("W", "acc_zero"), 1)
                        dve.wait_ge(*at("W", "acc_zero", 1))
                    if p == 2:
                        V.memset(aux[:, :], 0.0).then_inc(S("D", "aux_zero"), 1)
                        dve.wait_ge(*at("D", "aux_zero", 1))

                    def one_hot(k, column, n, numbers):
                        return V.tensor_tensor(
                            hot[k][:, 0:n, :], numbers[:, :].unsqueeze(1).to_broadcast([P, n, W]),
                            rel[:, ds(column, n)].unsqueeze(2).to_broadcast([P, n, W]), ALU.is_equal)

                    def sum_hot(k, n):
                        return V.tensor_reduce(hot_sum[k][:, :], hot[k][:, 0:n, :].rearrange("p c w -> p w c"), AX.X, ALU.add)

                    def add_window(target, columns, sums):
                        return V.tensor_tensor(target[:, columns], target[:, columns], sums, ALU.add)

                    def agg(t, i, k, p=p):
                        after(dve, *at(p, "sums_ready", t - 1))
                        one_hot(k, t * CH, chunks(t), node).then_inc(S(p, "hot_ready"), 1)
                        if p == 0:
                            dve.wait_ge(*at(p, "hot_ready", t + 1))
                            sum_hot(k, chunks(t)).then_inc(S(p, "aux_in"), 1)

                    def weigh(t, i, k, p=p):
                        if last_steps(p, t):
                            return
                        n = chunks(t)
                        dve.wait_ge(*at(p, "window_ready", t + 1))
                        V.tensor_tensor(hot[k][:, 0:n, :], hot[k][:, 0:n, :],
                                        rows[k][:, 0:n, F:F + 1].to_broadcast([P, n, W]), ALU.mult)\
                            .then_inc(S(p, "weighted"), 1)
                        dve.wait_ge(*at(p, "weighted", t + 1))
                        sum_hot(k, n).then_inc(S(p, "aux_in"), 1)

                    def add(t, i, k, p=p):
                        base = dve.value_load(base_i[0:1, ds(t, 1)], min_val=0, max_val=NP)
                        after(dve, *at(p, "sums_added", t))
                        dve.wait_ge(*at(p, "window_ready" if p in AUX else "sums_ready", t + 1))
                        add_window(acc, ds(base, W), win[k][:, 0:W]).then_inc(S(p, "sums_added"), 1)
                        if p in AUX:
                            after(dve, *at(p, "aux_added", t))
                            dve.wait_ge(*at(p, "sums_ready", t + 1))
                            add_window(aux, ds(base, W), auxp[0:1, 0:W]).then_inc(S(p, "aux_added"), 1)

                    def sweep(s, p=p):
                        def window(w):
                            n = s * WINDOWS + w
                            dve.wait_ge(*at(p, "g_numbered", n + 1))
                            one_hot(0, s * CH, CH, node_w).then_inc(S(p, "g_hot_ready"), 1)
                            dve.wait_ge(*at(p, "g_sums_ready", n + 1))
                            if p in AUX:
                                add_window(aux, ds(w * W, W), auxp[0:1, 0:W])
                            add_window(acc, ds(w * W, W), win[0][:, 0:W]).then_inc(S(p, "g_added"), 1)

                        V.tensor_scalar(node_w[:, :], node[:, :], base_all[:, ds(s, 1)], None, ALU.subtract)\
                            .then_inc(S(p, "g_numbered"), 1)
                        window(0)
                        with dve.Fori(1, WINDOWS) as w:
                            V.tensor_scalar(node_w[:, :], node_w[:, :], float(W), None, ALU.add)\
                                .then_inc(S(p, "g_numbered"), 1)
                            window(w)

                    def dense(t, i, k, p=p):
                        tile_acc = acc[:, ds(t * P, P)]
                        if not general:
                            done = min(t + LAG, STEPS) if isinstance(t, int) else t + LAG
                            dve.wait_ge(*at(p, "sums_added", done))
                            if p == 3:
                                dve.wait_ge(*at(p, "aux_added", done))
                        if p == 3:
                            dve.wait_ge(*at(p, "h_transposed", t + 1))
                            V.tensor_tensor(aT[:, :], tile_acc, trp[:, 0:P], ALU.add)
                            V.tensor_tensor(aux_t[:, :], aux[:, ds(t * P, P)], trp[0:1, P:2 * P], ALU.add)\
                                .then_inc(S(p, "aT_ready"), 1)
                        else:
                            V.tensor_scalar(aT[:, :], tile_acc, 1.0, None, ALU.mult).then_inc(S(p, "aT_ready"), 1)
                        dve.wait_ge(*at(p, "aT_ready", t + 1))
                        V.tensor_scalar(tile_acc, zero[:, :], 1.0, None, ALU.mult).then_inc(S(p, "acc_zeroed"), 1)
                        n_in = 1 if X_IN[p] is None else 2
                        dve.wait_ge(*at(p, f"in_loaded{k}", 16 * n_in * (i + 1)))
                        if X_OUT[p] is not None:
                            after(dve, *at(p, f"x_stored{k}", 16 * i))
                        if p == 0:
                            dve.wait_ge(*at(p, "rz_ready", t + 1))
                            V.tensor_tensor(gate_a[:, :], rz[:, 0:F], big[:, 3 * F:4 * F], ALU.mult).then_inc(S(p, "r_hn"), 1)
                            dve.wait_ge(*at(p, "r_hn", t + 1))
                            V.tensor_tensor(gate_b[:, :], gate_a[:, :], big[:, 2 * F:3 * F], ALU.add).then_inc(S(p, "cand_in"), 1)
                            dve.wait_ge(*at(p, "cand_ready", t + 1))
                            V.tensor_tensor(gate_a[:, :], h_t[k][:, 0:F], cand[:, :], ALU.subtract).then_inc(S(p, "h_less_n"), 1)
                            dve.wait_ge(*at(p, "h_less_n", t + 1))
                            V.tensor_tensor(gate_b[:, :], rz[:, F:2 * F], gate_a[:, :], ALU.mult).then_inc(S(p, "z_part"), 1)
                            dve.wait_ge(*at(p, "z_part", t + 1))
                            V.tensor_tensor(gate_a[:, :], gate_b[:, :], cand[:, :], ALU.add).then_inc(S(p, "gru_out"), 1)
                            dve.wait_ge(*at(p, "gru_out", t + 1))
                            V.tensor_tensor(xo_t[k][:, :], gate_a[:, :], x_t[k][:, :], ALU.add).then_inc(S(p, "x_ready"), 1)
                        if p == 1:
                            dve.wait_ge(*at(p, "products", t + 1))
                            V.tensor_scalar(gate_a[:, :], auxp[:, 0:F], rdeg[:, ds(t, 1)], None, ALU.mult).then_inc(S(p, "mean"), 1)
                            dve.wait_ge(*at(p, "mean", t + 1))
                            V.tensor_tensor(gate_b[:, :], gate_a[:, :], auxp[:, F:2 * F], ALU.add).then_inc(S(p, "mean_h"), 1)
                            dve.wait_ge(*at(p, "mean_h", t + 1))
                            V.scalar_tensor_tensor(out=xo_t[k][:, :], in0=gate_b[:, :], scalar=0.0, in1=x_t[k][:, :],
                                                   op0=ALU.max, op1=ALU.add).then_inc(S(p, "x_ready"), 1)
                        if p == 2:
                            dve.wait_ge(*at(p, "products", t + 1))
                            V.scalar_tensor_tensor(out=xo_t[k][:, :], in0=big[:, 0:F], scalar=0.0, in1=x_t[k][:, :],
                                                   op0=ALU.max, op1=ALU.add).then_inc(S(p, "x_ready"), 1)
                        if p in (0, 1, 2):
                            dve.wait_ge(*at(p, "x_ready", t + 1))
                            if p == 2:
                                after(dve, *at(p, f"h_stored{k}", 16 * i))
                                V.tensor_scalar(ho_t[k][:, F:ROW3], ones[:, 0:ROW3 - F], dinv[:, ds(t, 1)], None, ALU.mult)\
                                    .then_inc(S(p, "dinv_set"), 1)
                            after(dve, *at(p, "h_ready", t - 1))
                            moments(p, t, k, xo_t[k][:, :])
                            normalise(p, t, k, dinv[:, ds(t, 1)] if p == 2 else None)
                        if p in (3, 4):
                            n, o, b_sb, a_sb = (HID, "dinv_b", b1_sb, a1_sb) if p == 3 else (F, "dinv_b", b2_sb, a2_sb)
                            dve.wait_ge(*at(p, "products", t + 1))
                            pre = big[:, 0:n]
                            if p == 4:
                                V.tensor_tensor(hid_b[:, 0:n], big[:, 0:n], h_t[k][:, 0:F], ALU.add).then_inc(S(p, "own_loop"), 1)
                                dve.wait_ge(*at(p, "own_loop", t + 1))
                                pre = hid_b[:, 0:n]
                            V.scalar_tensor_tensor(out=hid_a[:, 0:n], in0=pre, scalar=dinv[:, ds(t, 1)], in1=b_sb,
                                                   op0=ALU.mult, op1=ALU.add).then_inc(S(p, "conv_out"), 1)
                            dve.wait_ge(*at(p, "conv_out", t + 1))
                            V.scalar_tensor_tensor(out=hid_b[:, 0:n], in0=hid_a[:, 0:n], scalar=0.0, in1=a_sb,
                                                   op0=ALU.min, op1=ALU.mult).then_inc(S(p, "below"), 1)
                            dve.wait_ge(*at(p, "below", t + 1))
                            V.scalar_tensor_tensor(out=hid_c[:, 0:n], in0=hid_a[:, 0:n], scalar=0.0, in1=hid_b[:, 0:n],
                                                   op0=ALU.max, op1=ALU.add).then_inc(S(p, "hid_ready"), 1)
                        if p == 4:
                            dve.wait_ge(*at(p, "hid_ready", t + 1))
                            V.tensor_tensor(xo_t[k][:, :], hid_c[:, 0:F], x_t[k][:, :], ALU.add).then_inc(S(p, "x_ready"), 1)

                    def typed_out(t, i, k, p=p):
                        dve.wait_ge(*at(p, "rows_all", t + 1))
                        after(dve, *at(p, f"rows_stored{k}", 16 * i))
                        V.tensor_copy(big_t[k][:, 8 * F:], big[:, 8 * F:]).then_inc(S(p, "rows_ready"), 1)

                    out_stage = [(LAG + 1, typed_out)] if p == 1 else []
                    if general:
                        with dve.Fori(0, STEPS) as s:
                            sweep(s)
                        dve.wait_ge(*at(p, "g_added", STEPS * WINDOWS))
                        all_tiles(dve, dense, *[stage for _, stage in out_stage])
                    else:
                        turns(dve, (1, add), (-1, agg), (LAG, dense), *[(0, weigh)] * (p == 3), *out_stage)

            by_order(dve, layers)


def kernel(x, src, dst, edge_type_16, edge_type_8, L0_gnn_message_W, L0_gnn_message_b, L0_gnn_gru_w_ih,
           L0_gnn_gru_w_hh, L0_gnn_gru_b_ih, L0_gnn_gru_b_hh, L1_gnn_W, L1_gnn_b, L2_gnn_relation_weights,
           L2_gnn_self_weight, L2_gnn_bias, L3_gnn_id, L3_gnn_W1, L3_gnn_b1, L3_gnn_a1, L3_gnn_W2, L3_gnn_b2,
           L3_gnn_a2):
    import numpy as _np
    import concourse.bacc as _bacc
    from concourse import mybir as _mybir
    from concourse.bass_utils import run_bass_kernel_spmd as _run

    def edges(a, fill):
        a = _np.asarray(a)
        a = _np.concatenate([a, _np.full(STEPS * CH * P - EDGES, fill, a.dtype)])
        return _np.ascontiguousarray(a.reshape(STEPS * CH, P).T)

    def rows_first(a):
        a = _np.asarray(a)
        return _np.ascontiguousarray(a.transpose(1, 0, 2).reshape(a.shape[1], -1))

    def turned(a):
        return _np.ascontiguousarray(_np.asarray(a).T)

    x = _np.asarray(x)
    given = [
        ("x", _np.concatenate([x, _np.zeros((NP - NODES, F), x.dtype)])),
        ("src", edges(src, NODES)), ("dst", edges(dst, NODES)),
        ("type8", edges(edge_type_8, 0)), ("type16", edges(edge_type_16, 0)),
        ("w_msg", rows_first(L0_gnn_message_W)), ("b_msg", _np.asarray(L0_gnn_message_b).reshape(-1)),
        ("w_ih", turned(L0_gnn_gru_w_ih)), ("w_hh", turned(L0_gnn_gru_w_hh)),
        ("b_ih", _np.asarray(L0_gnn_gru_b_ih)), ("b_hh", _np.asarray(L0_gnn_gru_b_hh)),
        ("w_l1", turned(L1_gnn_W)), ("b_l1", _np.asarray(L1_gnn_b)),
        ("w_rel", rows_first(L2_gnn_relation_weights)), ("w_self", _np.asarray(L2_gnn_self_weight)),
        ("b_l2", _np.asarray(L2_gnn_bias)), ("id_vec", _np.asarray(L3_gnn_id)),
        ("w1", _np.asarray(L3_gnn_W1)), ("b1", _np.asarray(L3_gnn_b1)), ("a1", _np.asarray(L3_gnn_a1)),
        ("w2", _np.asarray(L3_gnn_W2)), ("b2", _np.asarray(L3_gnn_b2)), ("a2", _np.asarray(L3_gnn_a2)),
    ]
    nc = _bacc.Bacc("TRN2", target_bir_lowering=False, num_devices=1)
    args = [nc.dram_tensor(f"in_{n}", a.shape, _mybir.dt.from_np(a.dtype), kind="ExternalInput").ap() for n, a in given]
    out = nc.dram_tensor("out_x", (NP, F), _mybir.dt.float32, kind="ExternalOutput").ap()
    gnn_layers(nc, *args, out)
    r = _run(nc, [{f"in_{n}": _np.ascontiguousarray(a) for n, a in given}], core_ids=[0])
    return r.results[0]["out_x"][:NODES]
```
